# Optimizing a Trainium2 kernel written in Bass

```python
import numpy as np
import jax
import jax.numpy as jnp

def _softmax(x, axis=-1):
    return jax.nn.softmax(x, axis=axis)

def _gelu(x):
    return jax.nn.gelu(x, approximate=True)

def _silu(x):
    return jax.nn.silu(x)

def _sigmoid(x):
    return jax.nn.sigmoid(x)

def _layernorm(x, axis=-1, eps=1e-05):
    m = jnp.mean(x, axis=axis, keepdims=True)
    v = jnp.var(x, axis=axis, keepdims=True)
    return (x - m) / jnp.sqrt(v + eps)

def _scatter_add(tgt, idx, src, axis=0):
    return tgt.at[idx].add(src)

def _segment_sum(src, seg, n):
    return jax.ops.segment_sum(src, seg, n)
kernel_name = 'mk_xattn_ffn_d1_seqx_r8_e9272f'

def setup_inputs(seed: int=0):
    np.random.seed(seed)
    _w = jnp.asarray

    def _rec_inputs():
        import jax
        import jax.numpy as jnp
        _rk = jax.random.key(seed)
        x = -0.0003929 + 0.9999 * jax.random.normal(jax.random.fold_in(_rk, 1), (4, 256, 512), jnp.float32)
        _lenS = 256 - jax.random.randint(jax.random.fold_in(_rk, 7), (4,), 0, max(1, 256 // 4) + 1, jnp.int32)
        _lenS2 = 1601 - jax.random.randint(jax.random.fold_in(_rk, 8), (4,), 0, max(1, 1601 // 4) + 1, jnp.int32)
        _ctx_4096P = jax.random.normal(jax.random.fold_in(_rk, 11), (4, 16, 512), jnp.float32)
        _ctx_4096c = jax.random.dirichlet(jax.random.fold_in(_rk, 511), 0.3 * jnp.ones((16,), jnp.float32), (4, 1601))
        _ctx_4096t = jnp.einsum('bsk,bkd->bsd', _ctx_4096c, _ctx_4096P)
        _ctx_4096t = _ctx_4096t * jax.lax.rsqrt(jnp.mean(jnp.square(_ctx_4096t)) + 1e-12) * 0.953939
        ctx_4096 = 2.81802e-05 + 1.00001 * (_ctx_4096t + 0.3 * jax.random.normal(jax.random.fold_in(_rk, 611), (4, 1601, 512), jnp.float32))
        _validS = jnp.arange(256)[None, :] < _lenS[:, None]
        _validS2 = jnp.arange(1601)[None, :] < _lenS2[:, None]
        _causal = jnp.tril(jnp.ones((256, 256), dtype=bool))
        mask_BxSxS2_ff0 = jnp.where(jnp.ones((4, 256, 1601), dtype=bool), 0.0, -1000000000.0).astype(jnp.float32)
        return (x, ctx_4096, mask_BxSxS2_ff0)
    x, ctx_4096, mask_BxSxS2_ff0 = _rec_inputs()

    def _L0_xattn_setup():
        import jax, jax.numpy as jnp
        import numpy as np
        BS, SEQ, D_MODEL = (4, 128, 512)
        N_Q_HEADS, N_KV_HEADS, D_K, D_V = (32, 8, 128, 128)
        ROPE_BASE = 10000.0

        def _rotate_half(x):
            x1, x2 = jnp.split(x, 2, axis=-1)
            return jnp.concatenate([-x2, x1], axis=-1)

        def _apply_rope(x, pos0):
            d = x.shape[-1]
            seq = x.shape[2]
            inv_freq = 1.0 / ROPE_BASE ** (jnp.arange(0, d, 2, dtype=jnp.float32) / d)
            pos = (pos0 + jnp.arange(seq)).astype(jnp.float32)
            ang = pos[:, None] * inv_freq[None, :]
            cos = jnp.concatenate([jnp.cos(ang), jnp.cos(ang)], axis=-1)
            sin = jnp.concatenate([jnp.sin(ang), jnp.sin(ang)], axis=-1)
            return x * cos[None, None] + _rotate_half(x) * sin[None, None]
        key = jax.random.key(seed)
        ks = jax.random.split(key, 8)
        w_scale = 0.02
        return {'query': jax.random.normal(ks[0], (BS, SEQ, D_MODEL), dtype=jnp.float32), 'key': jax.random.normal(ks[1], (BS, SEQ, D_MODEL), dtype=jnp.float32), 'value': jax.random.normal(ks[2], (BS, SEQ, D_MODEL), dtype=jnp.float32), 'mask': jnp.zeros((BS, SEQ, SEQ), dtype=jnp.float32), 'wq': jax.random.normal(ks[3], (D_MODEL, N_Q_HEADS * D_K), dtype=jnp.float32) * w_scale, 'wk': jax.random.normal(ks[4], (D_MODEL, N_KV_HEADS * D_K), dtype=jnp.float32) * w_scale, 'wv': jax.random.normal(ks[5], (D_MODEL, N_KV_HEADS * D_V), dtype=jnp.float32) * w_scale, 'wo': jax.random.normal(ks[6], (N_Q_HEADS * D_V, D_MODEL), dtype=jnp.float32) * w_scale, 'curr_seq_pos': 0}
    _L0_xattn_all = _L0_xattn_setup()
    _L0_xattn_in = {k: v for k, v in _L0_xattn_all.items() if k in ('wq', 'wk', 'wv', 'wo')}
    del _L0_xattn_all

    def _L0_ffn_setup():
        import jax, jax.numpy as jnp
        import numpy as np
        B, T, D_IN, D_OUT = (8, 256, 512, 512)
        N_LORAS, RANK = (16, 32)
        SCALING = 1.0
        key = jax.random.key(seed)
        ks = jax.random.split(key, 8)
        std = 1.0 / D_IN ** 0.5
        x = jax.random.normal(ks[0], (B, T, D_IN), dtype=jnp.float32)
        idx = jax.random.randint(ks[1], (B,), 0, N_LORAS)
        gate = jax.nn.one_hot(idx, N_LORAS, dtype=jnp.float32)
        kernel = jax.random.normal(ks[2], (D_IN, D_OUT), dtype=jnp.float32) * std
        bias = jnp.zeros((D_OUT,), dtype=jnp.float32)
        lora_A = jax.random.normal(ks[3], (N_LORAS, RANK, D_IN), dtype=jnp.float32) * std
        lora_B = jax.random.normal(ks[4], (N_LORAS, D_OUT, RANK), dtype=jnp.float32) * 0.01
        lora_A_shared = jax.random.normal(ks[5], (RANK, D_IN), dtype=jnp.float32) * std
        lora_B_shared = jax.random.normal(ks[6], (D_OUT, RANK), dtype=jnp.float32) * 0.01
        return {'x': x, 'gate': gate, 'kernel': kernel, 'bias': bias, 'lora_A': lora_A, 'lora_B': lora_B, 'lora_A_shared': lora_A_shared, 'lora_B_shared': lora_B_shared}
    _L0_ffn_all = _L0_ffn_setup()
    _L0_ffn_in = {k: v for k, v in _L0_ffn_all.items() if k in ('gate', 'kernel', 'bias', 'lora_A', 'lora_B', 'lora_A_shared', 'lora_B_shared')}
    del _L0_ffn_all
    return {'x': x, 'ctx_4096': ctx_4096, 'mask_BxSxS2_ff0': mask_BxSxS2_ff0, 'L0_xattn_wq': _L0_xattn_in['wq'], 'L0_xattn_wk': _L0_xattn_in['wk'], 'L0_xattn_wv': _L0_xattn_in['wv'], 'L0_xattn_wo': _L0_xattn_in['wo'], 'L0_ffn_gate': _L0_ffn_in['gate'], 'L0_ffn_kernel': _L0_ffn_in['kernel'], 'L0_ffn_bias': _L0_ffn_in['bias'], 'L0_ffn_lora_A': _L0_ffn_in['lora_A'], 'L0_ffn_lora_B': _L0_ffn_in['lora_B'], 'L0_ffn_lora_A_shared': _L0_ffn_in['lora_A_shared'], 'L0_ffn_lora_B_shared': _L0_ffn_in['lora_B_shared']}

def reference(x, ctx_4096, mask_BxSxS2_ff0, L0_xattn_wq, L0_xattn_wk, L0_xattn_wv, L0_xattn_wo, L0_ffn_gate, L0_ffn_kernel, L0_ffn_bias, L0_ffn_lora_A, L0_ffn_lora_B, L0_ffn_lora_A_shared, L0_ffn_lora_B_shared):
    import jax
    import jax.numpy as jnp

    def _L0_xattn_ref(query, key, value, mask, wq, wk, wv, wo, curr_seq_pos):
        import jax, jax.numpy as jnp
        import numpy as np
        BS, SEQ, D_MODEL = (4, 128, 512)
        N_Q_HEADS, N_KV_HEADS, D_K, D_V = (32, 8, 128, 128)
        ROPE_BASE = 10000.0

        def _rotate_half(x):
            x1, x2 = jnp.split(x, 2, axis=-1)
            return jnp.concatenate([-x2, x1], axis=-1)

        def _apply_rope(x, pos0):
            d = x.shape[-1]
            seq = x.shape[2]
            inv_freq = 1.0 / ROPE_BASE ** (jnp.arange(0, d, 2, dtype=jnp.float32) / d)
            pos = (pos0 + jnp.arange(seq)).astype(jnp.float32)
            ang = pos[:, None] * inv_freq[None, :]
            cos = jnp.concatenate([jnp.cos(ang), jnp.cos(ang)], axis=-1)
            sin = jnp.concatenate([jnp.sin(ang), jnp.sin(ang)], axis=-1)
            return x * cos[None, None] + _rotate_half(x) * sin[None, None]
        bs, sq, _ = query.shape
        n_groups = N_Q_HEADS // N_KV_HEADS
        q = (query @ wq).reshape(bs, sq, N_Q_HEADS, D_K).transpose((0, 2, 1, 3))
        sk = key.shape[1]
        k = (key @ wk).reshape(bs, sk, N_KV_HEADS, 1, D_K)
        k = jnp.repeat(k, n_groups, axis=3).reshape(bs, sk, N_Q_HEADS, D_K).transpose((0, 2, 1, 3))
        v = (value @ wv).reshape(bs, sk, N_KV_HEADS, 1, D_V)
        v = jnp.repeat(v, n_groups, axis=3).reshape(bs, sk, N_Q_HEADS, D_V).transpose((0, 2, 1, 3))
        scale = jnp.sqrt(jnp.float32(D_K))
        q = _apply_rope(q, curr_seq_pos)
        k = _apply_rope(k, curr_seq_pos)
        raw = jnp.einsum('bhqd,bhkd->bhqk', q, k) / scale
        masked = raw + mask[:bs, None, curr_seq_pos:curr_seq_pos + sq, :sk]
        attn = jax.nn.softmax(masked, axis=-1)
        out = jnp.einsum('bhqk,bhkd->bhqd', attn, v)
        out = out.transpose((0, 2, 1, 3)).reshape(bs, sq, N_Q_HEADS * D_V)
        return out @ wo

    def _L0_ffn_ref(x, gate, kernel, bias, lora_A, lora_B, lora_A_shared, lora_B_shared):
        import jax, jax.numpy as jnp
        import numpy as np
        B, T, D_IN, D_OUT = (8, 256, 512, 512)
        N_LORAS, RANK = (16, 32)
        SCALING = 1.0
        base_out = jnp.matmul(x, kernel) + bias
        b = gate.shape[0]
        x_flat = x.reshape(b, -1, x.shape[-1])
        A_eff = jnp.einsum('bn,nri->bri', gate, lora_A)
        B_eff = jnp.einsum('bn,nor->bor', gate, lora_B)
        Ax = jnp.einsum('bri,bti->btr', A_eff, x_flat)
        delta_flat = jnp.einsum('bor,btr->bto', B_eff, Ax)
        Ax_s = jnp.einsum('ri,bti->btr', lora_A_shared, x_flat)
        delta_flat = delta_flat + jnp.einsum('or,btr->bto', lora_B_shared, Ax_s)
        delta = delta_flat.reshape(x.shape[:-1] + (kernel.shape[-1],))
        return base_out + (SCALING * delta).astype(base_out.dtype)
    x = x + _L0_xattn_ref(_layernorm(x, axis=-1), ctx_4096, ctx_4096, mask_BxSxS2_ff0, L0_xattn_wq, L0_xattn_wk, L0_xattn_wv, L0_xattn_wo, 0)
    x = x + _L0_ffn_ref(_layernorm(x, axis=-1), L0_ffn_gate, L0_ffn_kernel, L0_ffn_bias, L0_ffn_lora_A, L0_ffn_lora_B, L0_ffn_lora_A_shared, L0_ffn_lora_B_shared)
    return x

_drawn_inputs = setup_inputs


def setup_inputs(seed=0):
    import zlib

    import numpy as np

    out = dict(_drawn_inputs(seed))
    spreads = {'L0_ffn_bias': (0.0, 0.1)}
    factors = {'L0_xattn_wq': 5.144, 'L0_xattn_wk': 5.138}
    for name, (base, spread) in spreads.items():
        noise = np.random.default_rng([zlib.crc32(name.encode()), seed]).standard_normal(out[name].shape)
        drawn = base * np.exp(spread * noise) if base else spread * noise
        out[name] = jnp.asarray(drawn.astype(out[name].dtype))
    for name, factor in factors.items():
        out[name] = (out[name] * factor).astype(out[name].dtype)
    return out
```

```python
from contextlib import ExitStack

import concourse.bass as bass
import concourse.mybir as mybir
from concourse.alu_op_type import AluOpType as ALU

F32 = mybir.dt.float32
F32R = mybir.dt.float32r
ACT = mybir.ActivationFunctionType
AX = mybir.AxisListType

P = 128
BATCH, SQ, DM = 4, 256, 512
SK = 1601
HEADS, KVH, DH = 32, 8, 128
HPG = HEADS // KVH
DC = DM // P
QT = SQ // P
NT = BATCH * QT
HW = HPG * P
SKP = SK + 1
KTILES = -(-SK // P)
KREM = SK - (KTILES - 1) * P
KCH = [(0, 402, 402), (402, 400, 400), (802, 400, 400), (1202, 400, 399)]
NCH = len(KCH)
VCH = [(s, min(512, SKP - s)) for s in range(0, SKP, 512)]
SCH = HPG * NCH
PARTS = [(0, 0), (0, 1), (1, 0)]
RING = 3
TV, TH = len(VCH), KTILES + 1
TG = TV + 2 * TH
TB = KTILES + KVH * TG
SPREAD = 11
LORAS, RANK = 16, 32
EPS = 1e-5
NEG_HUGE = -3.4e38


def key_rows(j):
    return KREM if j == KTILES - 1 else P


def query_stage(nc, sem, x, wq, cos_q, sin_q, q_scratch):
    CH = HPG * NT // 4
    PAIRS = KVH // 2
    with ExitStack() as ctx:
        sb = lambda name, shape, dt=F32: ctx.enter_context(nc.sbuf_tensor(name, shape, dt))
        ps = lambda name: ctx.enter_context(nc.psum_tensor(name, [P, 512], F32))
        ident = sb("q_ident", [P, P])
        xt = sb("q_x", [P, NT, DM])
        xn = sb("q_norm", [P, NT, DM])
        stats = sb("q_stats", [P, NT, 6])
        mean_var = sb("q_mean_var", [P, NT, 2])
        var_eps = sb("q_var_eps", [P, NT])
        minus_half = sb("q_minus_half", [P, NT])
        rstd = sb("q_rstd", [P, NT])
        cos_t = sb("q_cos", [P, 512])
        sin_t = sb("q_sin", [P, 512])
        xT_hl = sb("q_xT_hl", [P, 2, DC, NT * P], F32R)
        w_raw = sb("q_w_raw", [P, 2, DC, HW])
        w_hl = sb("q_w_hl", [P, 2, 2, DC, HW], F32R)
        rot = sb("q_rot", [P, 2, 512])
        straight = sb("q_straight", [P, 2, 512])
        q_out = sb("q_out", [P, 2, NT, 2, HW], F32R)
        t_bank = [ps(f"q_t{i}") for i in range(2)]
        q_bank = [ps(f"q_q{i}") for i in range(4)]

        x_in, tab_in = sem("q_x_in"), sem("q_tab_in")
        w_in = [sem(f"q_w_in{i}") for i in range(2)]
        ident_set, ident_done, half_set = sem("q_ident_set"), sem("q_ident_done"), sem("q_half_set")
        stat_done, aggr_done, veps_done = sem("q_stat_done"), sem("q_aggr_done"), sem("q_veps_done")
        rstd_done, xn_done = sem("q_rstd_done"), sem("q_xn_done")
        t_filled, t_hi, t_lo = sem("q_t_filled"), sem("q_t_hi"), sem("q_t_lo")
        w_hi, w_lo = sem("q_w_hi"), sem("q_w_lo")
        q_filled, q_mul, q_sum = sem("q_q_filled"), sem("q_q_mul"), sem("q_q_sum")
        q_hi, q_lo = sem("q_q_hi"), sem("q_q_lo")
        q_stored = [sem(f"q_stored{i}") for i in range(2)]

        wq_v = wq.rearrange("(c p) n -> p c n", p=P)
        MUL_CREDIT, LO_CREDIT, FILLED_CREDIT = len(q_bank), 2, 2 * CH
        block = ctx.enter_context(nc.Block())

        @block.sync
        def _(sp):
            sp.dma_start(xt[:, :, :], x.rearrange("b (t p) d -> p (b t) d", p=P)).then_inc(x_in, 16)
            sp.dma_start(cos_t[:, :], cos_q).then_inc(tab_in, 16)
            sp.dma_start(sin_t[:, :], sin_q).then_inc(tab_in, 16)
            for s in range(2):
                sp.dma_start(w_raw[:, s, :, :], wq_v[:, :, s * HW:(s + 1) * HW]).then_inc(w_in[s], 16)

            def store(group, s):
                sp.wait_ge(q_lo, (group + 1) * CH + LO_CREDIT)
                sp.dma_start(q_scratch[bass.ds(group, 1), :, :, :].rearrange("o n p w -> p (o n) w").bitcast(F32),
                             q_out[:, s, :, :, :].rearrange("p n h w -> p n (h w)").bitcast(F32)).then_inc(q_stored[s], 16)

            with sp.Fori(0, PAIRS - 1) as pair:
                for s in range(2):
                    group = pair * 2 + s
                    sp.wait_ge(w_lo, group + 1)
                    sp.dma_start(w_raw[:, s, :, :], wq_v[:, :, bass.ds((group + 2) * HW, HW)]).then_inc(w_in[s], 16)
                    store(group, s)
            for s in range(2):
                store(KVH - 2 + s, s)
            for s in range(2):
                sp.wait_ge(q_stored[s], 16 * (PAIRS + 1))

        @block.gpsimd
        def _(pool):
            pool.memset(ident[:, :], 0.0).then_inc(ident_set, 1)
            pool.memset(minus_half[:, :], -0.5).then_inc(half_set, 1)
            pool.sem_inc(q_lo, LO_CREDIT)
            pool.wait_ge(ident_set, 1)
            pool.affine_select(out=ident[:, :], in_=ident[:, :], compare_op=ALU.not_equal, fill=1.0,
                               base=0, pattern=[[-1, P]], channel_multiplier=1).then_inc(ident_done, 1)
            pool.wait_ge(half_set, 1)
            pool.wait_ge(veps_done, 1)
            pool.tensor_tensor(out=rstd[:, :], in0=var_eps[:, :], in1=minus_half[:, :], op=ALU.pow).then_inc(rstd_done, 1)

            def weights_lo(group, s):
                pool.wait_ge(w_hi, group + 1)
                pool.tensor_tensor(out=w_hl[:, s, 1, :, :], in0=w_raw[:, s, :, :],
                                   in1=w_hl[:, s, 0, :, :].bitcast(F32), op=ALU.subtract).then_inc(w_lo, 1)

            def queries_lo(group, s, last=False):
                for c in range(CH):
                    hh, tc = divmod(c, 2)
                    if c == CH // 2 and not last:
                        weights_lo(group + 1, 1 - s)
                    pool.wait_ge(q_hi, group * CH + c + 1)
                    pool.tensor_tensor(
                        out=q_out[:, s, tc * 4:tc * 4 + 4, 1, hh * P:(hh + 1) * P],
                        in0=rot[:, c % 2, :].rearrange("p (n q) -> p n q", q=P),
                        in1=q_out[:, s, tc * 4:tc * 4 + 4, 0, hh * P:(hh + 1) * P].bitcast(F32),
                        op=ALU.subtract).then_inc(q_lo, 1)

            weights_lo(0, 0)
            with pool.Fori(0, PAIRS - 1) as pair:
                for s in range(2):
                    queries_lo(pair * 2 + s, s)
            queries_lo(KVH - 2, 0)
            queries_lo(KVH - 1, 1, last=True)

        @block.scalar
        def _(act):
            for s in range(2):
                act.sem_inc(q_stored[s], 16)

            def weights_hi(group, s, turn):
                act.wait_ge(w_in[s], 16 * (turn + 1))
                act.wait_ge(q_filled, (group - 1) * CH + FILLED_CREDIT)
                act.activation(w_hl[:, s, 0, :, :], w_raw[:, s, :, :], ACT.Copy).then_inc(w_hi, 1)

            def queries_hi(pair, s, last=False):
                group = pair * 2 + s
                act.wait_ge(q_stored[s], 16 * (pair + 1))
                for c in range(CH):
                    hh, tc = divmod(c, 2)
                    if c == CH // 2 and not last:
                        weights_hi(group + 1, 1 - s, pair + s)
                    act.wait_ge(q_sum, group * CH + c + 1)
                    act.activation(q_out[:, s, tc * 4:tc * 4 + 4, 0, hh * P:(hh + 1) * P],
                                   rot[:, c % 2, :].rearrange("p (n q) -> p n q", q=P), ACT.Copy).then_inc(q_hi, 1)

            weights_hi(0, 0, 0)
            for n in range(NT):
                act.wait_ge(t_filled, n + 1)
                act.activation(xT_hl[:, 0, :, n * P:(n + 1) * P],
                               t_bank[n % 2][:, :].rearrange("p (c q) -> p c q", q=P), ACT.Copy).then_inc(t_hi, 1)
            with act.Fori(0, PAIRS - 1) as pair:
                for s in range(2):
                    queries_hi(pair, s)
            queries_hi(PAIRS - 1, 0)
            queries_hi(PAIRS - 1, 1, last=True)

        @block.vector
        def _(dve):
            dve.sem_inc(q_mul, MUL_CREDIT)
            dve.wait_ge(x_in, 16)
            for n in range(NT):
                dve.bn_stats(stats[:, n, :], xt[:, n, :]).then_inc(stat_done, 1)
            for n in range(NT):
                dve.wait_ge(stat_done, n + 1)
                dve.bn_aggr(mean_var[:, n, :], stats[:, n, :]).then_inc(aggr_done, 1)
            dve.wait_ge(aggr_done, NT)
            dve.tensor_scalar(var_eps[:, :], mean_var[:, :, 1], EPS, None, ALU.add).then_inc(veps_done, 1)
            dve.wait_ge(rstd_done, 1)
            for n in range(NT):
                dve.tensor_scalar(xn[:, n, :], xt[:, n, :], mean_var[:, n, 0:1], rstd[:, n:n + 1],
                                  ALU.subtract, ALU.mult).then_inc(xn_done, 1)
            for n in range(NT):
                dve.wait_ge(t_hi, n + 1)
                dve.tensor_tensor(out=xT_hl[:, 1, :, n * P:(n + 1) * P],
                                  in0=t_bank[n % 2][:, :].rearrange("p (c q) -> p c q", q=P),
                                  in1=xT_hl[:, 0, :, n * P:(n + 1) * P].bitcast(F32),
                                  op=ALU.subtract).then_inc(t_lo, 1)
            dve.wait_ge(tab_in, 32)
            with dve.Fori(0, PAIRS) as pair:
                for s in range(2):
                    for c in range(CH):
                        i = (pair * 2 + s) * CH + c
                        bank, r = q_bank[c % 4], c % 2
                        dve.wait_ge(q_filled, i + 1 + FILLED_CREDIT)
                        dve.wait_ge(q_lo, i - 1 + LO_CREDIT)
                        dve.tensor_tensor(out=rot[0:64, r, :], in0=bank[64:128, :], in1=sin_t[64:128, :], op=ALU.mult)
                        dve.tensor_tensor(out=rot[64:128, r, :], in0=bank[0:64, :], in1=sin_t[0:64, :], op=ALU.mult)
                        dve.tensor_tensor(out=straight[:, r, :], in0=bank[:, :], in1=cos_t[:, :], op=ALU.mult).then_inc(q_mul, 1)
                        dve.wait_ge(q_mul, i + 1 + MUL_CREDIT)
                        dve.tensor_tensor(out=rot[:, r, :], in0=rot[:, r, :], in1=straight[:, r, :], op=ALU.add).then_inc(q_sum, 1)

        @block.tensor
        def _(pe):
            pe.sem_inc(q_filled, FILLED_CREDIT)
            pe.wait_ge(ident_done, 1)
            for n in range(NT):
                pe.wait_ge(xn_done, n + 1)
                if n >= 2:
                    pe.wait_ge(t_lo, n - 1)
                for c in range(DC):
                    last = pe.transpose(t_bank[n % 2][:, c * P:(c + 1) * P], xn[:, n, c * P:(c + 1) * P], ident[:, :])
                last.then_inc(t_filled, 1)
            pe.wait_ge(t_lo, NT)
            with pe.Fori(0, PAIRS) as pair:
                for s in range(2):
                    group = pair * 2 + s
                    pe.wait_ge(w_lo, group + 1)
                    for c in range(CH):
                        hh, tc = divmod(c, 2)
                        bank = q_bank[c % 4]
                        pe.wait_ge(q_mul, group * CH + c - 3 + MUL_CREDIT)
                        steps = [(a, b, k) for a, b in PARTS for k in range(DC)]
                        for a, b, k in steps:
                            last = pe.matmul(bank[:, :], w_hl[:, s, a, k, hh * P:(hh + 1) * P],
                                             xT_hl[:, b, k, tc * 512:(tc + 1) * 512],
                                             start=(a, b, k) == steps[0], stop=(a, b, k) == steps[-1])
                        last.then_inc(q_filled, 1)


def attention_stage(nc, sem, ctx_in, mask, wk, wv, cos_k, sin_k, q_scratch, o_scratch):
    with ExitStack() as ctx:
        sb = lambda name, shape, dt=F32: ctx.enter_context(nc.sbuf_tensor(name, shape, dt))
        ps = lambda name: ctx.enter_context(nc.psum_tensor(name, [P, 512], F32))
        ident = sb("a_ident", [P, P])
        cos_t = sb("a_cos", [P, SKP])
        sin_t = sb("a_sin", [P, SKP])
        ctx_raw = sb("a_ctx_raw", [P, RING, DM])
        ctxT_hl = sb("a_ctxT_hl", [P, 2, DC, SKP], F32R)
        mask_t = sb("a_mask", [P, QT, SK])
        wk_raw = sb("a_wk_raw", [P, DC, DH])
        wv_raw = sb("a_wv_raw", [P, DC, DH])
        wk_hl = sb("a_wk_hl", [P, 2, DC, DH], F32R)
        wv_hl = sb("a_wv_hl", [P, 2, DC, DH], F32R)
        vT = sb("a_vT", [P, 2, 512])
        v_hl = sb("a_v_hl", [P, 2, KTILES, DH], F32R)
        rot = sb("a_rot", [P, KCH[0][1]])
        straight = sb("a_straight", [P, KCH[0][1]])
        kT_hl = sb("a_kT_hl", [P, 2, SKP], F32R)
        qT_hl = sb("a_qT_hl", [P, QT, 2, HW], F32R)
        probs = sb("a_probs", [P, QT, HPG, SK])
        pT_hl = sb("a_pT_hl", [P, RING, 2, HW], F32R)
        chunk_max = sb("a_chunk_max", [P, QT, HPG, NCH])
        neg_max = sb("a_neg_max", [P, QT, HPG])
        part_sum = sb("a_part_sum", [P, QT, HPG, 2])
        row_sum = sb("a_row_sum", [P, HPG])
        inv_sum = sb("a_inv_sum", [P, HPG])
        inv_wide = sb("a_inv_wide", [P, HPG, P])
        inv_rows = sb("a_inv_rows", [P, HW])
        oT = sb("a_oT", [P, QT, HW])
        s_bank = [ps(f"a_s{i}") for i in range(2)]
        t_bank = [ps(f"a_t{i}") for i in range(RING)]
        p_bank = [ps(f"a_p{i}") for i in range(2)]
        o_bank = ps("a_o")

        tab_in = sem("a_tab_in")
        ident_set, ident_done = sem("a_ident_set"), sem("a_ident_done")
        pad_set = sem("a_pad_set")
        ctx_loaded = [sem(f"a_ctx_loaded{i}") for i in range(RING)]
        mask_in = [sem(f"a_mask_in{t}") for t in range(QT)]
        q_in = [sem(f"a_q_in{t}") for t in range(QT)]
        wk_in, wv_in = sem("a_wk_in"), sem("a_wv_in")
        wk_hi, wk_lo, wv_hi, wv_lo = sem("a_wk_hi"), sem("a_wk_lo"), sem("a_wv_hi"), sem("a_wv_lo")
        p_filled, vT_done = sem("a_p_filled"), sem("a_vT_done")
        k_mul, k_sum, k_hi, k_lo = sem("a_k_mul"), sem("a_k_sum"), sem("a_k_hi"), sem("a_k_lo")
        t_filled, t_hi, t_lo = sem("a_t_filled"), sem("a_t_hi"), sem("a_t_lo")
        s_filled, s_read = sem("a_s_filled"), sem("a_s_read")
        max_done, exp_done = sem("a_max_done"), sem("a_exp_done")
        sum_done, inv_done, wide_done = sem("a_sum_done"), sem("a_inv_done"), sem("a_wide_done")
        pv_done = sem("a_pv_done")
        dve_passed, pool_passed = sem("a_dve_passed"), sem("a_pool_passed")
        o_stored = [sem(f"a_o_stored{t}") for t in range(QT)]
        READ_CREDIT = 2

        chunks_at = [[k for k in range(SCH) if k * SPREAD // SCH == j] for j in range(KTILES)]
        exp_at = [[] for _ in range(KTILES + 1)]
        for u in range(HPG):
            ready = ((u + 1) * NCH - 1) * SPREAD // SCH
            for part in range(2):
                exp_at[min(ready + 1 + part, KTILES)].append((u, part))
        EXP_PARTS = [(0, 802), (802, SK)]

        def t_base(b, hg):
            return (b + 1) * KTILES + hg * TG

        def over_heads(eng, prologue, head):
            prologue()
            with eng.Fori(0, BATCH - 1) as b:
                with eng.Fori(0, KVH - 1) as g:
                    head(b, g, b * KVH + g, "inner")
                head(b, KVH - 1, b * KVH + KVH - 1, "next batch")
            with eng.Fori(0, KVH - 1) as g:
                head(BATCH - 1, g, g + (BATCH - 1) * KVH, "inner")
            head(BATCH - 1, KVH - 1, BATCH * KVH - 1, "end")

        block = ctx.enter_context(nc.Block())

        @block.sync
        def _(sp):
            def load_ctx(b, j):
                rows = key_rows(j)
                sp.dma_start(ctx_raw[0:rows, j % RING, :],
                             ctx_in[bass.ds(b, 1), j * P:j * P + rows, :].rearrange("o p d -> (o p) d")
                             ).then_inc(ctx_loaded[j % RING], 16)

            def load_w(w, raw, done, g):
                sp.dma_start(raw[:, :, :], w.rearrange("(c p) n -> p c n", p=P)[:, :, bass.ds(g * DH, DH)]).then_inc(done, 16)

            def load_q(b, g, t):
                src = q_scratch[bass.ds(g, 1), bass.ds(b * QT + t, 1), :, :].rearrange("a o p w -> (a o p) w")
                sp.dma_start(qT_hl[:, t, :, :].rearrange("p h w -> p (h w)").bitcast(F32), src.bitcast(F32)).then_inc(q_in[t], 16)

            def load_mask(b, t):
                sp.dma_start(mask_t[:, t, :], mask[bass.ds(b, 1), t * P:(t + 1) * P, :].rearrange("o p k -> (o p) k")
                             ).then_inc(mask_in[t], 16)

            def store_o(b, g, t):
                dst = o_scratch[bass.ds(g, 1), bass.ds(b * QT + t, 1), :, :].rearrange("a o p w -> (a o p) w")
                sp.dma_start(dst, oT[:, t, :]).then_inc(o_stored[t], 16)

            def prologue():
                for t in range(QT):
                    sp.sem_inc(o_stored[t], 16)
                for j in range(RING):
                    load_ctx(0, j)
                load_w(wk, wk_raw, wk_in, 0)
                sp.dma_start(cos_t[:, :], cos_k).then_inc(tab_in, 16)
                sp.dma_start(sin_t[:, :], sin_k).then_inc(tab_in, 16)
                load_w(wv, wv_raw, wv_in, 0)
                for t in range(QT):
                    load_q(0, 0, t)
                    load_mask(0, t)
                for j in range(RING, KTILES):
                    sp.wait_ge(t_filled, j - RING + 1)
                    load_ctx(0, j)

            def head(b, g, hg, kind):
                T0 = t_base(b, hg)
                nb, ng = (b, g + 1) if kind == "inner" else (b + 1, 0)
                if kind != "end":
                    sp.wait_ge(wk_lo, hg + 1)
                    load_w(wk, wk_raw, wk_in, ng)
                    sp.wait_ge(s_filled, (2 * hg + 1) * SCH)
                    load_q(nb, ng, 0)
                    sp.wait_ge(wv_lo, hg + 1)
                    load_w(wv, wv_raw, wv_in, ng)
                if kind == "next batch":
                    sp.wait_ge(s_read, (2 * hg + 1) * SCH + READ_CREDIT)
                    load_mask(nb, 0)
                    for j in range(RING):
                        sp.wait_ge(t_filled, T0)
                        load_ctx(nb, j)
                sp.wait_ge(t_lo, T0 + TV + TH)
                store_o(b, g, 0)
                if kind != "end":
                    sp.wait_ge(s_filled, (2 * hg + 2) * SCH)
                    load_q(nb, ng, 1)
                T1 = T0 + TV + TH
                if kind == "next batch":
                    sp.wait_ge(s_read, (2 * hg + 2) * SCH + READ_CREDIT)
                    load_mask(nb, 1)
                    for j in range(RING, KTILES):
                        sp.wait_ge(t_filled, T1 + j - RING + 1)
                        load_ctx(nb, j)
                    T1 = T1 + KTILES
                sp.wait_ge(t_lo, T1 + TH)
                store_o(b, g, 1)

            over_heads(sp, prologue, head)
            for t in range(QT):
                sp.wait_ge(o_stored[t], 16 * (BATCH * KVH + 1))

        @block.gpsimd
        def _(pool):
            def split(raw, hl, loaded, hi, lo, hg):
                pool.wait_ge(loaded, 16 * (hg + 1))
                pool.sem_inc(pool_passed, 1)
                pool.tensor_copy(hl[:, 0, :, :], raw[:, :, :]).then_inc(hi, 1)
                pool.wait_ge(hi, hg + 1)
                pool.tensor_tensor(out=hl[:, 1, :, :], in0=raw[:, :, :], in1=hl[:, 0, :, :].bitcast(F32),
                                   op=ALU.subtract).then_inc(lo, 1)

            def keys_lo(hg):
                for c, (start, width, _) in enumerate(KCH):
                    pool.wait_ge(k_hi, hg * NCH + c + 1)
                    pool.tensor_tensor(out=kT_hl[:, 1, start:start + width], in0=rot[:, 0:width],
                                       in1=kT_hl[:, 0, start:start + width].bitcast(F32), op=ALU.subtract).then_inc(k_lo, 1)

            def widen(n):
                pool.wait_ge(inv_done, n + 1)
                pool.sem_inc(pool_passed, 1)
                pool.tensor_copy(inv_wide[:, :, :], inv_sum[:, :].unsqueeze(2).to_broadcast([P, HPG, P])).then_inc(wide_done, 1)

            def prologue():
                pool.memset(ident[:, :], 0.0).then_inc(ident_set, 1)
                pool.wait_ge(ident_set, 1)
                pool.affine_select(out=ident[:, :], in_=ident[:, :], compare_op=ALU.not_equal, fill=1.0,
                                   base=0, pattern=[[-1, P]], channel_multiplier=1).then_inc(ident_done, 1)
                pool.memset(ctxT_hl[:, :, :, SK:SKP].bitcast(F32), 0.0).then_inc(pad_set, 1)
                split(wk_raw, wk_hl, wk_in, wk_hi, wk_lo, 0)
                split(wv_raw, wv_hl, wv_in, wv_hi, wv_lo, 0)
                keys_lo(0)

            def head(b, g, hg, kind):
                T0 = t_base(b, hg)
                if kind != "end":
                    pool.wait_ge(p_filled, 2 * NCH * hg + NCH)
                    split(wk_raw, wk_hl, wk_in, wk_hi, wk_lo, hg + 1)
                    pool.wait_ge(p_filled, 2 * NCH * hg + 2 * NCH)
                    split(wv_raw, wv_hl, wv_in, wv_hi, wv_lo, hg + 1)
                pool.wait_ge(t_filled, T0)
                widen(hg * 2)
                if kind != "end":
                    keys_lo(hg + 1)
                pool.wait_ge(t_filled, T0 + TV + TH)
                widen(hg * 2 + 1)

            over_heads(pool, prologue, head)

        @block.scalar
        def _(act):
            def exps(n, t, step):
                for u, part in exp_at[step]:
                    lo, hi = EXP_PARTS[part]
                    act.wait_ge(max_done, n * HPG + u + 1)
                    act.activation(probs[:, t, u, lo:hi], probs[:, t, u, lo:hi], ACT.Exp, bias=neg_max[:, t, u:u + 1],
                                   accum_out=part_sum[:, t, u, part:part + 1]).then_inc(exp_done, 1)

            def half(n, T, t, more):
                def high(j):
                    act.wait_ge(t_filled, T + j + 1)
                    if j >= RING:
                        act.wait_ge(pv_done, n * KTILES + j - RING + 1)
                    rows = key_rows(j)
                    act.activation(pT_hl[0:rows, j % RING, 0, :], t_bank[j % RING][0:rows, :], ACT.Copy).then_inc(t_hi, 1)

                high(0)
                for j in range(KTILES):
                    if j + 1 < KTILES:
                        high(j + 1)
                    else:
                        act.wait_ge(t_filled, T + KTILES + 1)
                        act.activation(inv_rows[:, :], t_bank[KTILES % RING][:, :], ACT.Copy).then_inc(t_hi, 1)
                    if more:
                        exps(n + 1, 1 - t, j)
                if more:
                    exps(n + 1, 1 - t, KTILES)

            def values(T, hg):
                def copy(c):
                    act.wait_ge(p_filled, 2 * NCH * hg + NCH + c + 1)
                    act.activation(vT[:, c % 2, 0:VCH[c][1]], p_bank[c % 2][:, 0:VCH[c][1]], ACT.Copy).then_inc(vT_done, 1)

                def high(c):
                    act.wait_ge(t_filled, T + c + 1)
                    if c < TV - 1:
                        act.activation(v_hl[:, 0, 4 * c:4 * c + 4, :], t_bank[c % RING][:, :].rearrange("p (j d) -> p j d", d=DH),
                                       ACT.Copy).then_inc(t_hi, 1)
                    else:
                        act.activation(v_hl[0:KREM, 0, KTILES - 1, :], t_bank[c % RING][0:KREM, 0:DH], ACT.Copy).then_inc(t_hi, 1)

                copy(0)
                for c in range(1, TV):
                    copy(c)
                    high(c - 1)
                high(TV - 1)

            def context(T):
                for j in range(KTILES):
                    rows = key_rows(j)
                    act.wait_ge(t_filled, T + j + 1)
                    act.activation(ctxT_hl[:, 0, :, j * P:j * P + rows],
                                   t_bank[j % RING][:, :].rearrange("p (c k) -> p c k", k=P)[:, :, 0:rows], ACT.Copy).then_inc(t_hi, 1)

            def keys(hg):
                for c, (start, width, _) in enumerate(KCH):
                    act.wait_ge(k_sum, hg * NCH + c + 1)
                    act.activation(kT_hl[:, 0, start:start + width], rot[:, 0:width], ACT.Copy).then_inc(k_hi, 1)

            def prologue():
                context(0)
                keys(0)
                for step in range(KTILES + 1):
                    exps(0, 0, step)

            def head(b, g, hg, kind):
                T = t_base(b, hg)
                values(T, hg)
                half(hg * 2, T + TV, 0, True)
                T = T + TV + TH
                if kind == "next batch":
                    context(T)
                    T = T + KTILES
                if kind != "end":
                    keys(hg + 1)
                half(hg * 2 + 1, T, 1, kind != "end")

            over_heads(act, prologue, head)

        @block.vector
        def _(dve):
            def read_scores(n, t, k):
                u, c = divmod(k, NCH)
                start, _, width = KCH[c]
                dve.wait_ge(s_filled, n * SCH + k + 1)
                dve.sem_inc(dve_passed, 1)
                dve.tensor_tensor_reduce(out=probs[:, t, u, start:start + width], in0=s_bank[k % 2][:, 0:width],
                                         in1=mask_t[:, t, start:start + width], scale=1.0, scalar=NEG_HUGE,
                                         op0=ALU.add, op1=ALU.max, accum_out=chunk_max[:, t, u, c:c + 1]).then_inc(s_read, 1)
                if c == NCH - 1:
                    dve.wait_ge(s_read, n * SCH + k + 1 + READ_CREDIT)
                    dve.tensor_reduce(neg_max[:, t, u:u + 1], chunk_max[:, t, u, :], AX.X, ALU.max, negate=True).then_inc(max_done, 1)

            def half(n, T, t, more, hg, b):
                def low(j):
                    rows = key_rows(j)
                    dve.wait_ge(t_hi, T + j + 1)
                    dve.tensor_tensor(out=pT_hl[0:rows, j % RING, 1, :], in0=t_bank[j % RING][0:rows, :],
                                      in1=pT_hl[0:rows, j % RING, 0, :].bitcast(F32), op=ALU.subtract).then_inc(t_lo, 1)

                dve.wait_ge(exp_done, (n + 1) * HPG * 2)
                dve.tensor_tensor(out=row_sum[:, :], in0=part_sum[:, t, :, 0], in1=part_sum[:, t, :, 1], op=ALU.add).then_inc(sum_done, 1)
                dve.wait_ge(sum_done, n + 1)
                dve.reciprocal(inv_sum[:, :], row_sum[:, :]).then_inc(inv_done, 1)
                low(0)
                if more == "same batch":
                    dve.wait_ge(mask_in[1 - t], 16 * (b + 1))
                elif more:
                    dve.wait_ge(mask_in[1 - t], 16 * (b + 2))
                for j in range(KTILES):
                    if more:
                        for k in chunks_at[j]:
                            read_scores(n + 1, 1 - t, k)
                    if j + 1 < KTILES:
                        low(j + 1)
                dve.wait_ge(t_hi, T + TH)
                dve.wait_ge(pv_done, (n + 1) * KTILES)
                dve.wait_ge(o_stored[t], 16 * (hg + 1))
                dve.tensor_tensor(out=oT[:, t, :], in0=o_bank[:, :], in1=inv_rows[:, :], op=ALU.mult).then_inc(t_lo, 1)

            def values(T):
                for c in range(TV):
                    dve.wait_ge(t_hi, T + c + 1)
                    if c < TV - 1:
                        dve.tensor_tensor(out=v_hl[:, 1, 4 * c:4 * c + 4, :], in0=t_bank[c % RING][:, :].rearrange("p (j d) -> p j d", d=DH),
                                          in1=v_hl[:, 0, 4 * c:4 * c + 4, :].bitcast(F32), op=ALU.subtract).then_inc(t_lo, 1)
                    else:
                        dve.tensor_tensor(out=v_hl[0:KREM, 1, KTILES - 1, :], in0=t_bank[c % RING][0:KREM, 0:DH],
                                          in1=v_hl[0:KREM, 0, KTILES - 1, :].bitcast(F32), op=ALU.subtract).then_inc(t_lo, 1)

            def context(T):
                for j in range(KTILES):
                    rows = key_rows(j)
                    dve.wait_ge(t_hi, T + j + 1)
                    dve.tensor_tensor(out=ctxT_hl[:, 1, :, j * P:j * P + rows],
                                      in0=t_bank[j % RING][:, :].rearrange("p (c k) -> p c k", k=P)[:, :, 0:rows],
                                      in1=ctxT_hl[:, 0, :, j * P:j * P + rows].bitcast(F32), op=ALU.subtract).then_inc(t_lo, 1)

            def keys(hg, first=False):
                for c, (start, width, _) in enumerate(KCH):
                    i = hg * NCH + c
                    bank = p_bank[c % 2]
                    dve.wait_ge(p_filled, hg * 2 * NCH + c + 1)
                    if not (first and c == 0):
                        dve.wait_ge(k_lo, i)
                    cols = slice(start, start + width)
                    dve.tensor_tensor(out=rot[0:64, 0:width], in0=bank[64:128, 0:width], in1=sin_t[64:128, cols], op=ALU.mult)
                    dve.tensor_tensor(out=rot[64:128, 0:width], in0=bank[0:64, 0:width], in1=sin_t[0:64, cols], op=ALU.mult)
                    dve.tensor_tensor(out=straight[:, 0:width], in0=bank[:, 0:width], in1=cos_t[:, cols], op=ALU.mult).then_inc(k_mul, 1)
                    dve.wait_ge(k_mul, i + 1)
                    dve.tensor_tensor(out=rot[:, 0:width], in0=rot[:, 0:width], in1=straight[:, 0:width], op=ALU.add).then_inc(k_sum, 1)

            def prologue():
                dve.sem_inc(s_read, READ_CREDIT)
                context(0)
                dve.wait_ge(tab_in, 32)
                keys(0, first=True)
                dve.wait_ge(mask_in[0], 16)
                for k in range(SCH):
                    read_scores(0, 0, k)

            def head(b, g, hg, kind):
                T = t_base(b, hg)
                values(T)
                half(hg * 2, T + TV, 0, "same batch", hg, b)
                T = T + TV + TH
                if kind == "next batch":
                    context(T)
                    T = T + KTILES
                if kind != "end":
                    keys(hg + 1)
                half(hg * 2 + 1, T, 1, {"inner": "same batch", "next batch": "next batch", "end": None}[kind], hg, b)

            over_heads(dve, prologue, head)

        @block.tensor
        def _(pe):
            def project(w_hl, bank, start, width):
                steps = [(a, b, k) for a, b in PARTS for k in range(DC)]
                for a, b, k in steps:
                    last = pe.matmul(bank[:, 0:width], w_hl[:, a, k, :], ctxT_hl[:, b, k, start:start + width],
                                     start=(a, b, k) == steps[0], stop=(a, b, k) == steps[-1])
                return last.then_inc(p_filled, 1)

            def scores(n, t, k):
                u, c = divmod(k, NCH)
                start, width, _ = KCH[c]
                pe.wait_ge(s_read, n * SCH + k - 1 + READ_CREDIT)
                for i, (a, b) in enumerate(PARTS):
                    last = pe.matmul(s_bank[k % 2][:, 0:width], qT_hl[:, t, a, u * P:(u + 1) * P],
                                     kT_hl[:, b, start:start + width], start=i == 0, stop=i == 2)
                last.then_inc(s_filled, 1)

            def half(n, T, t, more, hg):
                def fill(i):
                    pe.wait_ge(t_lo, T + max(0, i - RING + 1))
                    bank = t_bank[i % RING]
                    if i == KTILES:
                        pe.wait_ge(wide_done, n + 1)
                        for u in range(HPG):
                            last = pe.transpose(bank[:, u * P:(u + 1) * P], inv_wide[:, u, :], ident[:, :])
                    else:
                        rows = key_rows(i)
                        for u in range(HPG):
                            last = pe.transpose(bank[0:rows, u * P:(u + 1) * P], probs[:, t, u, i * P:i * P + rows], ident[:, :])
                    last.then_inc(t_filled, 1)

                pe.wait_ge(exp_done, (n + 1) * HPG * 2)
                fill(0)
                fill(1)
                if more:
                    pe.wait_ge(q_in[1 - t], 16 * (hg + 1 + t))
                    if t == 1:
                        pe.wait_ge(k_lo, (hg + 2) * NCH)
                for j in range(KTILES):
                    if j + 2 <= KTILES:
                        fill(j + 2)
                    if more:
                        for k in chunks_at[j]:
                            scores(n + 1, 1 - t, k)
                    rows = key_rows(j)
                    pe.wait_ge(t_lo, T + j + 1)
                    for i, (a, b) in enumerate(PARTS):
                        last = pe.matmul(o_bank[:, :], v_hl[0:rows, a, j, :], pT_hl[0:rows, j % RING, b, :],
                                         start=j == 0 and i == 0, stop=j == KTILES - 1 and i == 2)
                    last.then_inc(pv_done, 1)

            def values(T, hg):
                def product(c):
                    start, width = VCH[c]
                    if c >= 2:
                        pe.wait_ge(vT_done, hg * TV + c - 1)
                    project(wv_hl, p_bank[c % 2], start, width)

                def turn(c):
                    pe.wait_ge(vT_done, hg * TV + c + 1)
                    pe.wait_ge(t_lo, T + max(0, c - RING + 1))
                    bank = t_bank[c % RING]
                    if c < TV - 1:
                        for i in range(4):
                            last = pe.transpose(bank[:, i * P:(i + 1) * P], vT[:, c % 2, i * P:(i + 1) * P], ident[:, :])
                    else:
                        last = pe.transpose(bank[0:KREM, 0:P], vT[:, c % 2, 0:KREM], ident[:, :])
                    last.then_inc(t_filled, 1)

                pe.wait_ge(wv_lo, hg + 1)
                product(0)
                for c in range(1, TV):
                    product(c)
                    turn(c - 1)
                turn(TV - 1)

            def context(T, b):
                for j in range(KTILES):
                    rows = key_rows(j)
                    slot = j % RING
                    tiles = len(range(slot, KTILES, RING))
                    pe.wait_ge(ctx_loaded[slot], 16 * (b * tiles + j // RING + 1))
                    if not (isinstance(T, int) and T == 0 and j < RING):
                        pe.wait_ge(t_lo, T + max(0, j - RING + 1))
                    bank = t_bank[slot]
                    for c in range(DC):
                        last = pe.transpose(bank[:, c * P:c * P + rows], ctx_raw[0:rows, slot, c * P:(c + 1) * P],
                                            ident[0:rows, 0:rows])
                    last.then_inc(t_filled, 1)

            def keys(hg, T):
                pe.wait_ge(t_lo, T)
                pe.wait_ge(wk_lo, hg + 1)
                for c, (start, width, _) in enumerate(KCH):
                    if c >= 2:
                        pe.wait_ge(k_mul, hg * NCH + c - 1)
                    project(wk_hl, p_bank[c % 2], start, width)

            def prologue():
                pe.wait_ge(ident_done, 1)
                context(0, 0)
                pe.wait_ge(pad_set, 1)
                keys(0, KTILES)
                pe.wait_ge(q_in[0], 16)
                pe.wait_ge(k_lo, NCH)
                for k in range(SCH):
                    scores(0, 0, k)

            def head(b, g, hg, kind):
                T = t_base(b, hg)
                values(T, hg)
                half(hg * 2, T + TV, 0, True, hg)
                T = T + TV + TH
                if kind == "next batch":
                    context(T, b + 1)
                    T = T + KTILES
                if kind != "end":
                    keys(hg + 1, T)
                half(hg * 2 + 1, T, 1, kind != "end", hg)

            over_heads(pe, prologue, head)


def projection_stage(nc, sem, x, wo, o_scratch, x2):
    PAIRS = KVH // 2
    with ExitStack() as ctx:
        sb = lambda name, shape, dt=F32: ctx.enter_context(nc.sbuf_tensor(name, shape, dt))
        w_raw = sb("p_w_raw", [P, 2, HPG, DM])
        w_hl = sb("p_w_hl", [P, 2, 2, HPG, DM], F32R)
        o_raw = sb("p_o_raw", [P, 2, NT, HW])
        o_hl = sb("p_o_hl", [P, 2, 2, NT, HW], F32R)
        xt = sb("p_x", [P, NT, DM])
        acc = [ctx.enter_context(nc.psum_tensor(f"p_acc{n}", [P, DM], F32)) for n in range(NT)]
        x_in = sem("p_x_in")
        w_in = [sem(f"p_w_in{s}") for s in range(2)]
        o_in = [sem(f"p_o_in{s}") for s in range(2)]
        w_hi, w_lo, o_hi, o_lo = sem("p_w_hi"), sem("p_w_lo"), sem("p_o_hi"), sem("p_o_lo")
        group_done = sem("p_group_done")
        x2_done = sem("p_x2_done")
        GROUP_CREDIT = 2

        wo_v = wo.rearrange("(g h p) n -> g p h n", p=P, h=HPG)
        block = ctx.enter_context(nc.Block())

        @block.sync
        def _(sp):
            def load(group, s):
                sp.dma_start(w_raw[:, s, :, :], wo_v[bass.ds(group, 1), :, :, :].rearrange("o p h n -> (o p) h n")).then_inc(w_in[s], 16)
                sp.dma_start(o_raw[:, s, :, :], o_scratch[bass.ds(group, 1), :, :, :].rearrange("o n p w -> p (o n) w")).then_inc(o_in[s], 16)

            for s in range(2):
                load(s, s)
            sp.dma_start(xt[:, :, :], x.rearrange("b (t p) d -> p (b t) d", p=P)).then_inc(x_in, 16)
            with sp.Fori(0, PAIRS - 1) as pair:
                for s in range(2):
                    group = pair * 2 + s
                    sp.wait_ge(w_lo, group + 1)
                    sp.wait_ge(o_lo, group + 1)
                    load(group + 2, s)

        @block.scalar
        def _(act):
            with act.Fori(0, PAIRS) as pair:
                for s in range(2):
                    group = pair * 2 + s
                    act.wait_ge(group_done, group - 1 + GROUP_CREDIT)
                    act.wait_ge(w_in[s], 16 * (pair + 1))
                    act.activation(w_hl[:, s, 0, :, :], w_raw[:, s, :, :], ACT.Copy).then_inc(w_hi, 1)
                    act.wait_ge(o_in[s], 16 * (pair + 1))
                    act.activation(o_hl[:, s, 0, :, :], o_raw[:, s, :, :], ACT.Copy).then_inc(o_hi, 1)

        @block.gpsimd
        def _(pool):
            with pool.Fori(0, PAIRS) as pair:
                for s in range(2):
                    pool.wait_ge(w_hi, pair * 2 + s + 1)
                    pool.tensor_tensor(out=w_hl[:, s, 1, :, :], in0=w_raw[:, s, :, :],
                                       in1=w_hl[:, s, 0, :, :].bitcast(F32), op=ALU.subtract).then_inc(w_lo, 1)

        @block.vector
        def _(dve):
            with dve.Fori(0, PAIRS) as pair:
                for s in range(2):
                    dve.wait_ge(o_hi, pair * 2 + s + 1)
                    dve.tensor_tensor(out=o_hl[:, s, 1, :, :], in0=o_raw[:, s, :, :],
                                      in1=o_hl[:, s, 0, :, :].bitcast(F32), op=ALU.subtract).then_inc(o_lo, 1)
            dve.wait_ge(x_in, 16)
            dve.wait_ge(group_done, KVH + GROUP_CREDIT)
            for n in range(NT):
                dve.tensor_tensor(out=x2[:, n, :], in0=acc[n][:, :], in1=xt[:, n, :], op=ALU.add).then_inc(x2_done, 1)
            dve.wait_ge(x2_done, NT)

        @block.tensor
        def _(pe):
            pe.sem_inc(group_done, GROUP_CREDIT)

            def group(pair, s, first=False, final=False):
                pe.wait_ge(w_lo, pair * 2 + s + 1)
                pe.wait_ge(o_lo, pair * 2 + s + 1)
                for hh in range(HPG):
                    for n in range(NT):
                        for i, (a, b) in enumerate(PARTS):
                            last = pe.matmul(acc[n][:, :], o_hl[:, s, a, n, hh * P:(hh + 1) * P], w_hl[:, s, b, hh, :],
                                             start=first and hh == 0 and i == 0, stop=final and hh == HPG - 1 and i == 2)
                last.then_inc(group_done, 1)

            group(0, 0, first=True)
            group(0, 1)
            with pe.Fori(1, PAIRS - 1) as pair:
                for s in range(2):
                    group(pair, s)
            group(PAIRS - 1, 0)
            group(PAIRS - 1, 1, final=True)


def dense_stage(nc, sem, kern, bias, gate_t, lora_a, lora_b_t, a_shared_t, b_shared_t, x2, out):
    NK = LORAS * RANK // P
    APK = P // RANK
    with ExitStack() as ctx:
        sb = lambda name, shape, dt=F32: ctx.enter_context(nc.sbuf_tensor(name, shape, dt))
        ident = sb("d_ident", [P, P])
        diag = sb("d_diag", [P, RANK])
        k_raw = sb("d_k_raw", [P, DC, DM])
        k_hl = sb("d_k_hl", [P, 2, DC, DM], F32R)
        bias_rows = sb("d_bias", [P, DM])
        x2_bias = sb("d_x2_bias", [P, NT, DM])
        a_raw = sb("d_a_raw", [P, NK, DM])
        asT_raw = sb("d_asT_raw", [P, DC, RANK])
        bsT_raw = sb("d_bsT_raw", [RANK, DM])
        gates = sb("d_gates", [P, NK, NT])
        G = sb("d_G", [P, NK, NT, RANK])
        bT = sb("d_bT", [P, NK, DM])
        asT_hl = sb("d_asT_hl", [P, 2, DC, RANK], F32R)
        bs_hl = sb("d_bs_hl", [RANK, 2, DM], F32R)
        aT_hl = sb("d_aT_hl", [P, 2, DC, NT * RANK], F32R)
        b_hl = sb("d_b_hl", [P, 2, 2, DM], F32R)
        stats = sb("d_stats", [P, NT, 6])
        mean_var = sb("d_mean_var", [P, NT, 2])
        var_eps = sb("d_var_eps", [P, NT])
        minus_half = sb("d_minus_half", [P, NT])
        rstd = sb("d_rstd", [P, NT])
        xn = sb("d_norm", [P, NT, DM])
        xT_hl = sb("d_xT_hl", [P, 2, DC, NT * P], F32R)
        ax_hl = sb("d_ax_hl", [P, 2, NT, P], F32R)
        axs_hl = sb("d_axs_hl", [RANK, 2, NT * P], F32R)
        y = sb("d_y", [P, NT, DM])
        bank = [ctx.enter_context(nc.psum_tensor(f"d_b{i}", [P, DM], F32)) for i in range(4)]
        y_bank = [ctx.enter_context(nc.psum_tensor(f"d_y{i}", [P, DM], F32)) for i in range(4)]

        lora_in, gates_in = sem("d_lora_in"), sem("d_gates_in")
        k_in, bias_in = sem("d_k_in"), sem("d_bias_in")
        ident_set, ident_done, half_set, zeroed = sem("d_ident_set"), sem("d_ident_done"), sem("d_half_set"), sem("d_zeroed")
        diag_done, G_done = sem("d_diag_done"), sem("d_G_done")
        k_hi, k_lo, xb_done = sem("d_k_hi"), sem("d_k_lo"), sem("d_xb_done")
        stat_done, aggr_done, veps_done = sem("d_stat_done"), sem("d_aggr_done"), sem("d_veps_done")
        rstd_done, xn_done = sem("d_rstd_done"), sem("d_xn_done")
        shared_hi, shared_lo = sem("d_shared_hi"), sem("d_shared_lo")
        filled, hi, lo = sem("d_filled"), sem("d_hi"), sem("d_lo")
        y_filled, y_done, stored = sem("d_y_filled"), sem("d_y_done"), sem("d_stored")

        F_AT, F_B, F_XT, F_AX, F_AXS = 0, 2, 4, 12, 14

        block = ctx.enter_context(nc.Block())

        @block.sync
        def _(sp):
            for n in range(APK):
                sp.dma_start(gates[n * RANK:(n + 1) * RANK, :, :],
                             gate_t.rearrange("(k n) b -> n k b", n=APK)[n:n + 1, :, :].to_broadcast([RANK, NK, NT])
                             ).then_inc(gates_in, 16)
            sp.dma_start(bT[:, :, :], lora_b_t.rearrange("n r o -> (n r) o").rearrange("(k p) o -> p k o", p=P)).then_inc(lora_in, 16)
            sp.dma_start(a_raw[:, :, :], lora_a.rearrange("n r i -> (n r) i").rearrange("(k p) i -> p k i", p=P)).then_inc(lora_in, 16)
            sp.dma_start(asT_raw[:, :, :], a_shared_t.rearrange("(c p) r -> p c r", p=P)).then_inc(lora_in, 16)
            sp.dma_start(bsT_raw[:, :], b_shared_t).then_inc(lora_in, 16)
            sp.dma_start(k_raw[:, :, :], kern.rearrange("(c p) n -> p c n", p=P)).then_inc(k_in, 16)
            sp.dma_start(bias_rows[:, :], bias.rearrange("(o n) -> o n", o=1).to_broadcast([P, DM])).then_inc(bias_in, 16)
            out_v = out.rearrange("b (t p) d -> (b t) p d", p=P)
            for n in range(NT):
                sp.wait_ge(y_done, n + 1)
                sp.dma_start(out_v[n, :, :], y[:, n, :]).then_inc(stored, 16)
            sp.wait_ge(stored, 16 * NT)

        @block.gpsimd
        def _(pool):
            pool.memset(ident[:, :], 0.0).then_inc(ident_set, 1)
            pool.memset(minus_half[:, :], -0.5).then_inc(half_set, 1)
            pool.wait_ge(ident_set, 1)
            pool.affine_select(out=ident[:, :], in_=ident[:, :], compare_op=ALU.not_equal, fill=1.0,
                               base=0, pattern=[[-1, P]], channel_multiplier=1).then_inc(ident_done, 1)
            pool.memset(ax_hl[:, :, :, :].bitcast(F32), 0.0).then_inc(zeroed, 1)
            pool.wait_ge(half_set, 1)
            pool.wait_ge(veps_done, 1)
            pool.tensor_tensor(out=rstd[:, :], in0=var_eps[:, :], in1=minus_half[:, :], op=ALU.pow).then_inc(rstd_done, 1)
            pool.wait_ge(k_hi, 1)
            pool.tensor_tensor(out=k_hl[:, 1, :, :], in0=k_raw[:, :, :], in1=k_hl[:, 0, :, :].bitcast(F32), op=ALU.subtract).then_inc(k_lo, 1)
            pool.wait_ge(bias_in, 16)
            for n in range(NT):
                pool.tensor_tensor(out=x2_bias[:, n, :], in0=x2[:, n, :], in1=bias_rows[:, :], op=ALU.add).then_inc(xb_done, 1)

        def drains():
            for i in range(2):
                yield F_AT + i, bank[(F_AT + i) % 4][:, :].rearrange("p (c m) -> p c m", c=2), [aT_hl[:, h, 2 * i:2 * i + 2, :] for h in range(2)]
            for i in range(2):
                yield F_B + i, bank[(F_B + i) % 4][:, :], [b_hl[:, h, i, :] for h in range(2)]
            for n in range(NT):
                yield F_XT + n, bank[(F_XT + n) % 4][:, :].rearrange("p (c q) -> p c q", q=P), [xT_hl[:, h, :, n * P:(n + 1) * P] for h in range(2)]
            for i in range(2):
                for q in range(APK):
                    rows = slice(q * RANK, (q + 1) * RANK)
                    yield F_AX + i, bank[(F_AX + i) % 4][rows, q * P:(q + 1) * P], [ax_hl[rows, h, 4 * i + q, :] for h in range(2)]
            for i in range(2):
                yield F_AXS + i, bank[(F_AXS + i) % 4][0:RANK, :], [axs_hl[:, h, 512 * i:512 * (i + 1)] for h in range(2)]

        @block.scalar
        def _(act):
            act.wait_ge(k_in, 16)
            act.activation(k_hl[:, 0, :, :], k_raw[:, :, :], ACT.Copy).then_inc(k_hi, 1)
            act.wait_ge(lora_in, 16 * 4)
            act.activation(asT_hl[:, 0, :, :], asT_raw[:, :, :], ACT.Copy).then_inc(shared_hi, 1)
            act.activation(bs_hl[:, 0, :], bsT_raw[:, :], ACT.Copy).then_inc(shared_hi, 1)
            act.wait_ge(zeroed, 1)
            for f, src, (high, _) in drains():
                act.wait_ge(filled, f + 1)
                act.activation(high, src, ACT.Copy).then_inc(hi, 1)

        @block.vector
        def _(dve):
            for n in range(NT):
                dve.bn_stats(stats[:, n, :], x2[:, n, :]).then_inc(stat_done, 1)
            for n in range(NT):
                dve.wait_ge(stat_done, n + 1)
                dve.bn_aggr(mean_var[:, n, :], stats[:, n, :]).then_inc(aggr_done, 1)
            dve.wait_ge(aggr_done, NT)
            dve.tensor_scalar(var_eps[:, :], mean_var[:, :, 1], EPS, None, ALU.add).then_inc(veps_done, 1)
            dve.wait_ge(ident_done, 1)
            for n in range(APK):
                rows = slice(n * RANK, (n + 1) * RANK)
                dve.tensor_copy(diag[rows, :], ident[rows, rows]).then_inc(diag_done, 1)
            dve.wait_ge(diag_done, APK)
            dve.wait_ge(gates_in, 16 * APK)
            dve.tensor_tensor(out=G[:, :, :, :].rearrange("p k b r -> p (k b) r"),
                              in0=gates[:, :, :].rearrange("p k b -> p (k b)").unsqueeze(2).to_broadcast([P, NK * NT, RANK]),
                              in1=diag[:, :].unsqueeze(1).to_broadcast([P, NK * NT, RANK]), op=ALU.mult).then_inc(G_done, 1)
            dve.wait_ge(shared_hi, 2)
            dve.tensor_tensor(out=asT_hl[:, 1, :, :], in0=asT_raw[:, :, :], in1=asT_hl[:, 0, :, :].bitcast(F32), op=ALU.subtract).then_inc(shared_lo, 1)
            dve.tensor_tensor(out=bs_hl[:, 1, :], in0=bsT_raw[:, :], in1=bs_hl[:, 0, :].bitcast(F32), op=ALU.subtract).then_inc(shared_lo, 1)
            dve.wait_ge(rstd_done, 1)
            for n in range(NT):
                dve.tensor_scalar(xn[:, n, :], x2[:, n, :], mean_var[:, n, 0:1], rstd[:, n:n + 1],
                                  ALU.subtract, ALU.mult).then_inc(xn_done, 1)
            for i, (f, src, (high, low)) in enumerate(drains()):
                dve.wait_ge(hi, i + 1)
                ins = dve.tensor_tensor(out=low, in0=src, in1=high.bitcast(F32), op=ALU.subtract)
                if f not in (F_AX, F_AX + 1) or (i - F_AX) % APK == APK - 1:
                    ins.then_inc(lo, 1)
            for n in range(NT):
                dve.wait_ge(y_filled, n + 1)
                dve.wait_ge(xb_done, n + 1)
                dve.tensor_tensor(out=y[:, n, :], in0=y_bank[n % 4][:, :], in1=x2_bias[:, n, :], op=ALU.add).then_inc(y_done, 1)

        @block.tensor
        def _(pe):
            def free(f):
                if f >= 4:
                    pe.wait_ge(lo, f - 3)

            def three(dst, stationary, moving, start=True, stop=True):
                for i, (a, b) in enumerate(PARTS):
                    last = pe.matmul(dst, stationary(a), moving(b), start=start and i == 0, stop=stop and i == 2)
                return last

            pe.wait_ge(ident_done, 1)
            pe.wait_ge(lora_in, 16 * 4)
            pe.wait_ge(G_done, 1)
            for i in range(2):
                free(F_AT + i)
                for cc in range(2):
                    c = 2 * i + cc
                    for k in range(NK):
                        last = pe.matmul(bank[(F_AT + i) % 4][:, cc * 256:(cc + 1) * 256], a_raw[:, k, c * P:(c + 1) * P],
                                         G[:, k, :, :].rearrange("p b r -> p (b r)"), start=k == 0, stop=k == NK - 1)
                last.then_inc(filled, 1)
            for i in range(2):
                free(F_B + i)
                for k in range(NK):
                    last = pe.matmul(bank[(F_B + i) % 4][:, :], G[:, k, i * APK:(i + 1) * APK, :].rearrange("p b r -> p (b r)"),
                                     bT[:, k, :], start=k == 0, stop=k == NK - 1)
                last.then_inc(filled, 1)
            for n in range(NT):
                pe.wait_ge(xn_done, n + 1)
                free(F_XT + n)
                for c in range(DC):
                    last = pe.transpose(bank[(F_XT + n) % 4][:, c * P:(c + 1) * P], xn[:, n, c * P:(c + 1) * P], ident[:, :])
                last.then_inc(filled, 1)
            for i in range(2):
                pe.wait_ge(lo, F_XT + 4 * i + 4)
                free(F_AX + i)
                for c in range(DC):
                    last = three(bank[(F_AX + i) % 4][:, :], lambda h: aT_hl[:, h, c, i * P:(i + 1) * P],
                                 lambda h: xT_hl[:, h, c, 512 * i:512 * (i + 1)], start=c == 0, stop=c == DC - 1)
                last.then_inc(filled, 1)
            for i in range(2):
                free(F_AXS + i)
                for c in range(DC):
                    last = three(bank[(F_AXS + i) % 4][0:RANK, :], lambda h: asT_hl[:, h, c, :],
                                 lambda h: xT_hl[:, h, c, 512 * i:512 * (i + 1)], start=c == 0, stop=c == DC - 1)
                last.then_inc(filled, 1)
            pe.wait_ge(k_lo, 1)
            pe.wait_ge(shared_lo, 2)
            for n in range(NT):
                if n >= 4:
                    pe.wait_ge(y_done, n - 3)
                if n == 0:
                    pe.wait_ge(lo, F_AXS + 1)
                if n == 4:
                    pe.wait_ge(lo, F_AXS + 2)
                tile = slice(n * P, (n + 1) * P)
                for c in range(DC):
                    three(y_bank[n % 4][:, :], lambda h: xT_hl[:, h, c, tile], lambda h: k_hl[:, h, c, :], start=c == 0, stop=False)
                three(y_bank[n % 4][:, :], lambda h: ax_hl[:, h, n, :], lambda h: b_hl[:, h, n // 4, :], start=False, stop=False)
                last = three(y_bank[n % 4][:, :], lambda h: axs_hl[:, h, tile], lambda h: bs_hl[:, h, :], start=False)
                last.then_inc(y_filled, 1)


def program(nc, x, context, mask, wq, wk, wv, wo, gate_t, kern, bias, lora_a, lora_b_t, a_shared_t, b_shared_t,
            cos_q, sin_q, cos_k, sin_k, out):
    with ExitStack() as ctx:
        sem = lambda name: ctx.enter_context(nc.semaphore(name))
        q_scratch = nc.dram_tensor("q_scratch", (KVH, NT, P, 2 * HW), F32R, kind="Internal").ap()
        o_scratch = nc.dram_tensor("o_scratch", (KVH, NT, P, HW), F32, kind="Internal").ap()
        query_stage(nc, sem, x, wq, cos_q, sin_q, q_scratch)
        attention_stage(nc, sem, context, mask, wk, wv, cos_k, sin_k, q_scratch, o_scratch)
        x2 = ctx.enter_context(nc.sbuf_tensor("x2", [P, NT, DM], F32))
        projection_stage(nc, sem, x, wo, o_scratch, x2)
        dense_stage(nc, sem, kern, bias, gate_t, lora_a, lora_b_t, a_shared_t, b_shared_t, x2, out)


def rotary_tables(np):
    f = np.float32
    inv_freq = f(1.0) / np.power(f(10000.0), np.arange(0, DH, 2, dtype=f) / f(DH))
    angle = np.arange(SKP, dtype=f)[None, :] * inv_freq[:, None]
    cos, sin = np.cos(angle.astype(np.float64)), np.sin(angle.astype(np.float64))
    cos, sin = np.concatenate([cos, cos]), np.concatenate([sin, -sin])
    scale = 1.0 / np.sqrt(float(DH))
    q = lambda a: np.tile(a[:, :SQ] * scale, (1, 512 // SQ)).astype(f)
    return q(cos), q(sin), cos.astype(f), sin.astype(f)


_INS = ["x", "ctx_4096", "mask_BxSxS2_ff0", "L0_xattn_wq", "L0_xattn_wk", "L0_xattn_wv", "L0_xattn_wo",
        "L0_ffn_gate", "L0_ffn_kernel", "L0_ffn_bias", "L0_ffn_lora_A", "L0_ffn_lora_B",
        "L0_ffn_lora_A_shared", "L0_ffn_lora_B_shared"]
_TABLES = ["cos_q", "sin_q", "cos_k", "sin_k"]


def kernel(**inputs):
    import numpy as np
    import concourse.bacc as bacc
    from concourse.bass_utils import run_bass_kernel_spmd

    nc = bacc.Bacc("TRN2", target_bir_lowering=False, num_devices=1)
    arrays, args = {}, []
    lay = {"L0_ffn_gate": (1, 0), "L0_ffn_lora_B": (0, 2, 1), "L0_ffn_lora_A_shared": (1, 0), "L0_ffn_lora_B_shared": (1, 0)}
    named = [(n, np.ascontiguousarray(np.transpose(inputs[n], lay.get(n, range(np.ndim(inputs[n])))))) for n in _INS] + list(zip(_TABLES, rotary_tables(np)))
    for name, a in named:
        arrays[f"in_{name}"] = a
        args.append(nc.dram_tensor(f"in_{name}", a.shape, mybir.dt.from_np(a.dtype), kind="ExternalInput").ap())
    args.append(nc.dram_tensor("out", (BATCH, SQ, DM), F32, kind="ExternalOutput").ap())
    program(nc, *args)
    r = run_bass_kernel_spmd(nc, [arrays], core_ids=[0])
    return r.results[0]["out"]
```

```python
from contextlib import ExitStack

import concourse.bass as bass
import concourse.mybir as mybir
from concourse.alu_op_type import AluOpType as ALU

F32 = mybir.dt.float32
F32R = mybir.dt.float32r
ACT = mybir.ActivationFunctionType
AX = mybir.AxisListType

P = 128
BATCH, SQ, DM = 4, 256, 512
SK = 1601
HEADS, KVH, DH = 32, 8, 128
HPG = HEADS // KVH
DC = DM // P
QT = SQ // P
NT = BATCH * QT
HW = HPG * P
SKP = SK + 1
KTILES = -(-SK // P)
KREM = SK - (KTILES - 1) * P
KCH = [(0, 402, 402), (402, 400, 400), (802, 400, 400), (1202, 400, 399)]
NCH = len(KCH)
SCH = HPG * NCH
PARTS = [(0, 0), (0, 1), (1, 0)]
RING = 3
TV, TH = -(-KTILES // 4), KTILES + 1
TG = TV + 2 * TH
LORAS, RANK = 16, 32
EPS = 1e-5
NEG_HUGE = -3.4e38


def key_rows(j):
    return KREM if j == KTILES - 1 else P


def query_stage(nc, sem, x, wq, cos_q, sin_q, q_scratch):
    CH = HPG * NT // 4
    PAIRS = KVH // 2
    with ExitStack() as ctx:
        sb = lambda name, shape, dt=F32: ctx.enter_context(nc.sbuf_tensor(name, shape, dt))
        ps = lambda name: ctx.enter_context(nc.psum_tensor(name, [P, 512], F32))
        ident = sb("q_ident", [P, P])
        xt = sb("q_x", [P, NT, DM])
        xn = sb("q_norm", [P, NT, DM])
        stats = sb("q_stats", [P, NT, 6])
        mean_var = sb("q_mean_var", [P, NT, 2])
        var_eps = sb("q_var_eps", [P, NT])
        minus_half = sb("q_minus_half", [P, NT])
        rstd = sb("q_rstd", [P, NT])
        cos_t = sb("q_cos", [P, 512])
        sin_t = sb("q_sin", [P, 512])
        xT_hl = sb("q_xT_hl", [P, 2, DC, NT * P], F32R)
        w_raw = sb("q_w_raw", [P, 2, DC, HW])
        w_hl = sb("q_w_hl", [P, 2, 2, DC, HW], F32R)
        rot = sb("q_rot", [P, 2, 512])
        straight = sb("q_straight", [P, 2, 512])
        q_out = sb("q_out", [P, 2, NT, 2, HW], F32R)
        t_bank = [ps(f"q_t{i}") for i in range(2)]
        q_bank = [ps(f"q_q{i}") for i in range(4)]

        x_in, tab_in = sem("q_x_in"), sem("q_tab_in")
        w_in = [sem(f"q_w_in{i}") for i in range(2)]
        ident_set, ident_done, half_set = sem("q_ident_set"), sem("q_ident_done"), sem("q_half_set")
        stat_done, aggr_done, veps_done = sem("q_stat_done"), sem("q_aggr_done"), sem("q_veps_done")
        rstd_done, xn_done = sem("q_rstd_done"), sem("q_xn_done")
        t_filled, t_hi, t_lo = sem("q_t_filled"), sem("q_t_hi"), sem("q_t_lo")
        w_hi, w_lo = sem("q_w_hi"), sem("q_w_lo")
        q_filled, q_mul, q_sum = sem("q_q_filled"), sem("q_q_mul"), sem("q_q_sum")
        q_hi, q_lo = sem("q_q_hi"), sem("q_q_lo")
        q_stored = [sem(f"q_stored{i}") for i in range(2)]

        wq_v = wq.rearrange("(c p) n -> p c n", p=P)
        MUL_CREDIT, LO_CREDIT, FILLED_CREDIT = len(q_bank), 2, 2 * CH
        block = ctx.enter_context(nc.Block())

        @block.sync
        def _(sp):
            sp.dma_start(xt[:, :, :], x.rearrange("b (t p) d -> p (b t) d", p=P)).then_inc(x_in, 16)
            sp.dma_start(cos_t[:, :], cos_q).then_inc(tab_in, 16)
            sp.dma_start(sin_t[:, :], sin_q).then_inc(tab_in, 16)
            for s in range(2):
                sp.dma_start(w_raw[:, s, :, :], wq_v[:, :, s * HW:(s + 1) * HW]).then_inc(w_in[s], 16)

            def store(group, s):
                sp.wait_ge(q_lo, (group + 1) * CH + LO_CREDIT)
                sp.dma_start(q_scratch[bass.ds(group, 1), :, :, :].rearrange("o n p w -> p (o n) w").bitcast(F32),
                             q_out[:, s, :, :, :].rearrange("p n h w -> p n (h w)").bitcast(F32)).then_inc(q_stored[s], 16)

            with sp.Fori(0, PAIRS - 1) as pair:
                for s in range(2):
                    group = pair * 2 + s
                    sp.wait_ge(w_lo, group + 1)
                    sp.dma_start(w_raw[:, s, :, :], wq_v[:, :, bass.ds((group + 2) * HW, HW)]).then_inc(w_in[s], 16)
                    store(group, s)
            for s in range(2):
                store(KVH - 2 + s, s)
            for s in range(2):
                sp.wait_ge(q_stored[s], 16 * (PAIRS + 1))

        @block.gpsimd
        def _(pool):
            pool.memset(ident[:, :], 0.0).then_inc(ident_set, 1)
            pool.memset(minus_half[:, :], -0.5).then_inc(half_set, 1)
            pool.sem_inc(q_lo, LO_CREDIT)
            pool.wait_ge(ident_set, 1)
            pool.affine_select(out=ident[:, :], in_=ident[:, :], compare_op=ALU.not_equal, fill=1.0,
                               base=0, pattern=[[-1, P]], channel_multiplier=1).then_inc(ident_done, 1)
            pool.wait_ge(half_set, 1)
            pool.wait_ge(veps_done, 1)
            pool.tensor_tensor(out=rstd[:, :], in0=var_eps[:, :], in1=minus_half[:, :], op=ALU.pow).then_inc(rstd_done, 1)

            def weights_lo(group, s):
                pool.wait_ge(w_hi, group + 1)
                pool.tensor_tensor(out=w_hl[:, s, 1, :, :], in0=w_raw[:, s, :, :],
                                   in1=w_hl[:, s, 0, :, :].bitcast(F32), op=ALU.subtract).then_inc(w_lo, 1)

            def queries_lo(group, s, last=False):
                for c in range(CH):
                    hh, tc = divmod(c, 2)
                    if c == CH // 2 and not last:
                        weights_lo(group + 1, 1 - s)
                    pool.wait_ge(q_hi, group * CH + c + 1)
                    pool.tensor_tensor(
                        out=q_out[:, s, tc * 4:tc * 4 + 4, 1, hh * P:(hh + 1) * P],
                        in0=rot[:, c % 2, :].rearrange("p (n q) -> p n q", q=P),
                        in1=q_out[:, s, tc * 4:tc * 4 + 4, 0, hh * P:(hh + 1) * P].bitcast(F32),
                        op=ALU.subtract).then_inc(q_lo, 1)

            weights_lo(0, 0)
            with pool.Fori(0, PAIRS - 1) as pair:
                for s in range(2):
                    queries_lo(pair * 2 + s, s)
            queries_lo(KVH - 2, 0)
            queries_lo(KVH - 1, 1, last=True)

        @block.scalar
        def _(act):
            for s in range(2):
                act.sem_inc(q_stored[s], 16)

            def weights_hi(group, s, turn):
                act.wait_ge(w_in[s], 16 * (turn + 1))
                act.wait_ge(q_filled, (group - 1) * CH + FILLED_CREDIT)
                act.activation(w_hl[:, s, 0, :, :], w_raw[:, s, :, :], ACT.Copy).then_inc(w_hi, 1)

            def queries_hi(pair, s, last=False):
                group = pair * 2 + s
                act.wait_ge(q_stored[s], 16 * (pair + 1))
                for c in range(CH):
                    hh, tc = divmod(c, 2)
                    if c == CH // 2 and not last:
                        weights_hi(group + 1, 1 - s, pair + s)
                    act.wait_ge(q_sum, group * CH + c + 1)
                    act.activation(q_out[:, s, tc * 4:tc * 4 + 4, 0, hh * P:(hh + 1) * P],
                                   rot[:, c % 2, :].rearrange("p (n q) -> p n q", q=P), ACT.Copy).then_inc(q_hi, 1)

            weights_hi(0, 0, 0)
            for n in range(NT):
                act.wait_ge(t_filled, n + 1)
                act.activation(xT_hl[:, 0, :, n * P:(n + 1) * P],
                               t_bank[n % 2][:, :].rearrange("p (c q) -> p c q", q=P), ACT.Copy).then_inc(t_hi, 1)
            with act.Fori(0, PAIRS - 1) as pair:
                for s in range(2):
                    queries_hi(pair, s)
            queries_hi(PAIRS - 1, 0)
            queries_hi(PAIRS - 1, 1, last=True)

        @block.vector
        def _(dve):
            dve.sem_inc(q_mul, MUL_CREDIT)
            dve.wait_ge(x_in, 16)
            for n in range(NT):
                dve.bn_stats(stats[:, n, :], xt[:, n, :]).then_inc(stat_done, 1)
            for n in range(NT):
                dve.wait_ge(stat_done, n + 1)
                dve.bn_aggr(mean_var[:, n, :], stats[:, n, :]).then_inc(aggr_done, 1)
            dve.wait_ge(aggr_done, NT)
            dve.tensor_scalar(var_eps[:, :], mean_var[:, :, 1], EPS, None, ALU.add).then_inc(veps_done, 1)
            dve.wait_ge(rstd_done, 1)
            for n in range(NT):
                dve.tensor_scalar(xn[:, n, :], xt[:, n, :], mean_var[:, n, 0:1], rstd[:, n:n + 1],
                                  ALU.subtract, ALU.mult).then_inc(xn_done, 1)
            for n in range(NT):
                dve.wait_ge(t_hi, n + 1)
                dve.tensor_tensor(out=xT_hl[:, 1, :, n * P:(n + 1) * P],
                                  in0=t_bank[n % 2][:, :].rearrange("p (c q) -> p c q", q=P),
                                  in1=xT_hl[:, 0, :, n * P:(n + 1) * P].bitcast(F32),
                                  op=ALU.subtract).then_inc(t_lo, 1)
            dve.wait_ge(tab_in, 32)
            with dve.Fori(0, PAIRS) as pair:
                for s in range(2):
                    for c in range(CH):
                        i = (pair * 2 + s) * CH + c
                        bank, r = q_bank[c % 4], c % 2
                        dve.wait_ge(q_filled, i + 1 + FILLED_CREDIT)
                        dve.wait_ge(q_lo, i - 1 + LO_CREDIT)
                        dve.tensor_tensor(out=rot[0:64, r, :], in0=bank[64:128, :], in1=sin_t[64:128, :], op=ALU.mult)
                        dve.tensor_tensor(out=rot[64:128, r, :], in0=bank[0:64, :], in1=sin_t[0:64, :], op=ALU.mult)
                        dve.tensor_tensor(out=straight[:, r, :], in0=bank[:, :], in1=cos_t[:, :], op=ALU.mult).then_inc(q_mul, 1)
                        dve.wait_ge(q_mul, i + 1 + MUL_CREDIT)
                        dve.tensor_tensor(out=rot[:, r, :], in0=rot[:, r, :], in1=straight[:, r, :], op=ALU.add).then_inc(q_sum, 1)

        @block.tensor
        def _(pe):
            pe.sem_inc(q_filled, FILLED_CREDIT)
            pe.wait_ge(ident_done, 1)
            for n in range(NT):
                pe.wait_ge(xn_done, n + 1)
                if n >= 2:
                    pe.wait_ge(t_lo, n - 1)
                for c in range(DC):
                    last = pe.transpose(t_bank[n % 2][:, c * P:(c + 1) * P], xn[:, n, c * P:(c + 1) * P], ident[:, :])
                last.then_inc(t_filled, 1)
            pe.wait_ge(t_lo, NT)
            with pe.Fori(0, PAIRS) as pair:
                for s in range(2):
                    group = pair * 2 + s
                    pe.wait_ge(w_lo, group + 1)
                    for c in range(CH):
                        hh, tc = divmod(c, 2)
                        bank = q_bank[c % 4]
                        pe.wait_ge(q_mul, group * CH + c - 3 + MUL_CREDIT)
                        steps = [(a, b, k) for a, b in PARTS for k in range(DC)]
                        for a, b, k in steps:
                            last = pe.matmul(bank[:, :], w_hl[:, s, a, k, hh * P:(hh + 1) * P],
                                             xT_hl[:, b, k, tc * 512:(tc + 1) * 512],
                                             start=(a, b, k) == steps[0], stop=(a, b, k) == steps[-1])
                        last.then_inc(q_filled, 1)


def attention_stage(nc, sem, ctx_t, mask, wk, wv, cos_k, sin_k, q_scratch, o_scratch):
    with ExitStack() as ctx:
        sb = lambda name, shape, dt=F32: ctx.enter_context(nc.sbuf_tensor(name, shape, dt))
        ps = lambda name: ctx.enter_context(nc.psum_tensor(name, [P, 512], F32))
        ident = sb("a_ident", [P, P])
        cos_t = sb("a_cos", [P, SKP])
        sin_t = sb("a_sin", [P, SKP])
        ctx_raw = sb("a_ctx_raw", [P, 2, KCH[0][1]])
        ctxT_hl = sb("a_ctxT_hl", [P, 2, DC, SKP], F32R)
        mask_t = sb("a_mask", [P, QT, SK])
        w_raw = sb("a_w_raw", [P, DC, DH])
        wk_hl = sb("a_wk_hl", [P, 2, DC, DH], F32R)
        wv_hl = sb("a_wv_hl", [P, 2, DC, DH], F32R)
        vT = sb("a_vT", [P, SKP])
        v_hl = sb("a_v_hl", [P, 2, KTILES, DH], F32R)
        rot = sb("a_rot", [P, 2, KCH[0][1]])
        straight = sb("a_straight", [P, 2, KCH[0][1]])
        kT_hl = sb("a_kT_hl", [P, 2, SKP], F32R)
        qT_hl = sb("a_qT_hl", [P, QT, 2, HW], F32R)
        probs = sb("a_probs", [P, QT, HPG, SK])
        pT_hl = sb("a_pT_hl", [P, RING, 2, HW], F32R)
        chunk_max = sb("a_chunk_max", [P, QT, HPG, NCH])
        neg_max = sb("a_neg_max", [P, QT, HPG])
        part_sum = sb("a_part_sum", [P, QT, HPG, 2])
        row_sum = sb("a_row_sum", [P, HPG])
        inv_sum = sb("a_inv_sum", [P, HPG])
        inv_wide = sb("a_inv_wide", [P, HPG, P])
        inv_rows = sb("a_inv_rows", [P, HW])
        oT = sb("a_oT", [P, QT, HW])
        s_bank = [ps(f"a_s{i}") for i in range(2)]
        t_bank = [ps(f"a_t{i}") for i in range(RING)]
        p_bank = [ps(f"a_p{i}") for i in range(2)]
        o_bank = ps("a_o")

        tab_in = sem("a_tab_in")
        ident_set, ident_done = sem("a_ident_set"), sem("a_ident_done")
        pad_set = sem("a_pad_set")
        ctx_loaded = [sem(f"a_ctx_loaded{i}") for i in range(2)]
        ctx_hi, ctx_lo = sem("a_ctx_hi"), sem("a_ctx_lo")
        mask_in = [sem(f"a_mask_in{t}") for t in range(QT)]
        q_in = [sem(f"a_q_in{t}") for t in range(QT)]
        w_in = sem("a_w_in")
        wk_hi, wk_lo, wv_hi, wv_lo = sem("a_wk_hi"), sem("a_wk_lo"), sem("a_wv_hi"), sem("a_wv_lo")
        p_filled, vT_done = sem("a_p_filled"), sem("a_vT_done")
        k_mul, k_sum, k_hi, k_lo = sem("a_k_mul"), sem("a_k_sum"), sem("a_k_hi"), sem("a_k_lo")
        t_filled, t_hi, t_lo = sem("a_t_filled"), sem("a_t_hi"), sem("a_t_lo")
        s_filled, s_read = sem("a_s_filled"), sem("a_s_read")
        max_done, exp_done = sem("a_max_done"), sem("a_exp_done")
        sum_done, inv_done, wide_done = sem("a_sum_done"), sem("a_inv_done"), sem("a_wide_done")
        pv_done = sem("a_pv_done")
        dve_passed, pool_passed = sem("a_dve_passed"), sem("a_pool_passed")
        o_stored = [sem(f"a_o_stored{t}") for t in range(QT)]
        READ_CREDIT = 2
        TURN_CREDIT = 1

        VOFF = [TV, 0]
        STEPS = [v + KTILES for v in VOFF]
        SUM_AT = 5
        FIRST_AT, LAST_AT = [0, 2], [s - 2 for s in STEPS]
        chunks_at = [[[k for k in range(SCH) if FIRST_AT[t] + k * (LAST_AT[t] - FIRST_AT[t]) // SCH == i]
                      for i in range(STEPS[t])] for t in range(QT)]
        EXP_PARTS = [(0, 802), (802, SK)]
        exp_at = [[[] for _ in range(STEPS[t] + 1)] for t in range(QT)]
        for t in range(QT):
            for u in range(HPG):
                ready = next(i for i in range(STEPS[t]) if u * NCH + NCH - 1 in chunks_at[t][i])
                for part in range(2):
                    exp_at[t][min(ready + 2 + part, STEPS[t])].append((u, part))
        PIECES = NCH * DC

        def piece(q):
            (start, width, real), c = KCH[q // DC], q % DC
            return c, start, real

        def t_base(hg):
            return hg * TG + TURN_CREDIT

        def over_heads(eng, prologue, head):
            prologue()
            with eng.Fori(0, BATCH - 1) as b:
                with eng.Fori(0, KVH - 1) as g:
                    head(b, g, b * KVH + g, "inner")
                head(b, KVH - 1, b * KVH + KVH - 1, "next batch")
            with eng.Fori(0, KVH - 1) as g:
                head(BATCH - 1, g, g + (BATCH - 1) * KVH, "inner")
            head(BATCH - 1, KVH - 1, BATCH * KVH - 1, "end")

        block = ctx.enter_context(nc.Block())

        @block.sync
        def _(sp):
            def load_ctx(b, q):
                c, start, real = piece(q)
                sp.dma_start(ctx_raw[:, q % 2, 0:real],
                             ctx_t[bass.ds(b, 1), c * P:(c + 1) * P, start:start + real].rearrange("o p k -> (o p) k")
                             ).then_inc(ctx_loaded[q % 2], 16)

            def load_w(w, g):
                sp.dma_start(w_raw[:, :, :], w.rearrange("(c p) n -> p c n", p=P)[:, :, bass.ds(g * DH, DH)]).then_inc(w_in, 16)

            def load_q(b, g, t):
                src = q_scratch[bass.ds(g, 1), bass.ds(b * QT + t, 1), :, :].rearrange("a o p w -> (a o p) w")
                sp.dma_start(qT_hl[:, t, :, :].rearrange("p h w -> p (h w)").bitcast(F32), src.bitcast(F32)).then_inc(q_in[t], 16)

            def load_mask(b, t):
                sp.dma_start(mask_t[:, t, :], mask[bass.ds(b, 1), t * P:(t + 1) * P, :].rearrange("o p k -> (o p) k")
                             ).then_inc(mask_in[t], 16)

            def store_o(b, g, t):
                dst = o_scratch[bass.ds(g, 1), bass.ds(b * QT + t, 1), :, :].rearrange("a o p w -> (a o p) w")
                sp.dma_start(dst, oT[:, t, :]).then_inc(o_stored[t], 16)

            def prologue():
                for t in range(QT):
                    sp.sem_inc(o_stored[t], 16)
                load_w(wk, 0)
                for q in range(2):
                    load_ctx(0, q)
                sp.dma_start(cos_t[:, :], cos_k).then_inc(tab_in, 16)
                sp.dma_start(sin_t[:, :], sin_k).then_inc(tab_in, 16)
                sp.wait_ge(wk_lo, 1)
                load_w(wv, 0)
                for q in range(2, PIECES):
                    sp.wait_ge(ctx_lo, q - 1)
                    load_ctx(0, q)
                for t in range(QT):
                    load_q(0, 0, t)
                    load_mask(0, t)

            def head(b, g, hg, kind):
                T = t_base(hg)
                nb, ng = (b, g + 1) if kind == "inner" else (b + 1, 0)
                if kind != "end":
                    sp.wait_ge(wv_lo, hg + 1)
                    load_w(wk, ng)
                    sp.wait_ge(s_filled, (2 * hg + 1) * SCH)
                    load_q(nb, ng, 0)
                if kind == "next batch":
                    for q in range(2):
                        sp.wait_ge(ctx_lo, (b + 1) * PIECES)
                        load_ctx(nb, q)
                    sp.wait_ge(s_read, (2 * hg + 1) * SCH + READ_CREDIT)
                    load_mask(nb, 0)
                if kind != "end":
                    sp.wait_ge(wk_lo, hg + 2)
                    load_w(wv, ng)
                if kind == "next batch":
                    for q in range(2, PIECES):
                        sp.wait_ge(ctx_lo, nb * PIECES + q - 1)
                        load_ctx(nb, q)
                if kind != "end":
                    sp.wait_ge(s_filled, (2 * hg + 2) * SCH)
                    load_q(nb, ng, 1)
                if kind == "next batch":
                    sp.wait_ge(s_read, (2 * hg + 2) * SCH + READ_CREDIT)
                    load_mask(nb, 1)
                sp.wait_ge(t_lo, T + TV + TH)
                store_o(b, g, 0)
                sp.wait_ge(t_lo, T + TG)
                store_o(b, g, 1)

            over_heads(sp, prologue, head)
            for t in range(QT):
                sp.wait_ge(o_stored[t], 16 * (BATCH * KVH + 1))

        @block.gpsimd
        def _(pool):
            def split(hl, hi, lo, hg, loads):
                pool.wait_ge(w_in, 16 * loads)
                pool.sem_inc(pool_passed, 1)
                pool.tensor_copy(hl[:, 0, :, :], w_raw[:, :, :]).then_inc(hi, 1)
                pool.wait_ge(hi, hg + 1)
                pool.tensor_tensor(out=hl[:, 1, :, :], in0=w_raw[:, :, :], in1=hl[:, 0, :, :].bitcast(F32),
                                   op=ALU.subtract).then_inc(lo, 1)

            def keys_lo(hg):
                for c, (start, width, _) in enumerate(KCH):
                    pool.wait_ge(k_hi, hg * NCH + c + 1)
                    pool.tensor_tensor(out=kT_hl[:, 1, start:start + width], in0=rot[:, c % 2, 0:width],
                                       in1=kT_hl[:, 0, start:start + width].bitcast(F32), op=ALU.subtract).then_inc(k_lo, 1)

            def widen(n):
                pool.wait_ge(inv_done, n + 1)
                pool.sem_inc(pool_passed, 1)
                pool.tensor_copy(inv_wide[:, :, :], inv_sum[:, :].unsqueeze(2).to_broadcast([P, HPG, P])).then_inc(wide_done, 1)

            def prologue():
                pool.memset(ident[:, :], 0.0).then_inc(ident_set, 1)
                pool.wait_ge(ident_set, 1)
                pool.affine_select(out=ident[:, :], in_=ident[:, :], compare_op=ALU.not_equal, fill=1.0,
                                   base=0, pattern=[[-1, P]], channel_multiplier=1).then_inc(ident_done, 1)
                pool.memset(ctxT_hl[:, :, :, SK:SKP].bitcast(F32), 0.0).then_inc(pad_set, 1)
                split(wk_hl, wk_hi, wk_lo, 0, 1)
                split(wv_hl, wv_hi, wv_lo, 0, 2)
                keys_lo(0)

            def head(b, g, hg, kind):
                T = t_base(hg)
                if kind != "end":
                    pool.wait_ge(p_filled, 2 * NCH * (hg + 1))
                    split(wk_hl, wk_hi, wk_lo, hg + 1, 2 * hg + 3)
                    split(wv_hl, wv_hi, wv_lo, hg + 1, 2 * hg + 4)
                pool.wait_ge(t_filled, T)
                widen(hg * 2)
                if kind != "end":
                    keys_lo(hg + 1)
                pool.wait_ge(t_filled, T + TV + TH)
                widen(hg * 2 + 1)

            over_heads(pool, prologue, head)

        @block.scalar
        def _(act):
            def exps(n, t, u, part):
                lo, hi = EXP_PARTS[part]
                act.wait_ge(max_done, n * HPG + u + 1)
                act.activation(probs[:, t, u, lo:hi], probs[:, t, u, lo:hi], ACT.Exp, bias=neg_max[:, t, u:u + 1],
                               accum_out=part_sum[:, t, u, part:part + 1]).then_inc(exp_done, 1)

            def context(b, q):
                c, start, real = piece(q)
                act.wait_ge(ctx_loaded[q % 2], 16 * (b * (PIECES // 2) + q // 2 + 1))
                act.activation(ctxT_hl[:, 0, c, start:start + real], ctx_raw[:, q % 2, 0:real], ACT.Copy).then_inc(ctx_hi, 1)

            def high(n, T, t, i):
                act.wait_ge(t_filled, T + i + 1)
                bank, j = t_bank[i % RING], i - VOFF[t]
                if j < -1:
                    act.activation(v_hl[:, 0, 4 * i:4 * i + 4, :], bank[:, :].rearrange("p (j d) -> p j d", d=DH),
                                   ACT.Copy).then_inc(t_hi, 1)
                elif j == -1:
                    act.activation(v_hl[0:KREM, 0, KTILES - 1, :], bank[0:KREM, 0:DH], ACT.Copy).then_inc(t_hi, 1)
                elif j < KTILES:
                    if j >= RING:
                        act.wait_ge(pv_done, n * KTILES + j - RING + 1)
                    rows = key_rows(j)
                    act.activation(pT_hl[0:rows, j % RING, 0, :], bank[0:rows, :], ACT.Copy).then_inc(t_hi, 1)
                else:
                    act.activation(inv_rows[:, :], bank[:, :], ACT.Copy).then_inc(t_hi, 1)

            def half(n, T, t, more, next_b, done=0):
                if not done:
                    high(n, T, t, 0)
                for i in range(STEPS[t]):
                    if i + 1 >= done:
                        high(n, T, t, i + 1)
                    if more:
                        for u, part in exp_at[t][i]:
                            exps(n + 1, 1 - t, u, part)
                    if next_b is not None and i < PIECES:
                        context(next_b, i)
                if more:
                    for u, part in exp_at[t][STEPS[t]]:
                        exps(n + 1, 1 - t, u, part)

            def keys(hg, T=None):
                for c, (start, width, _) in enumerate(KCH):
                    if c == NCH - 2 and T is not None:
                        high(hg * 2 - 1, T, 1, 0)
                        high(hg * 2 - 1, T, 1, 1)
                    act.wait_ge(k_sum, hg * NCH + c + 1)
                    act.activation(kT_hl[:, 0, start:start + width], rot[:, c % 2, 0:width], ACT.Copy).then_inc(k_hi, 1)
                    if c == NCH - 2 and T is not None:
                        high(hg * 2 - 1, T, 1, 2)

            def values(hg):
                for c, (start, width, _) in enumerate(KCH):
                    act.wait_ge(p_filled, (2 * hg + 1) * NCH + c + 1)
                    act.activation(vT[:, start:start + width], p_bank[c % 2][:, 0:width], ACT.Copy).then_inc(vT_done, 1)

            def prologue():
                for q in range(PIECES):
                    context(0, q)
                keys(0)
                for u in range(HPG):
                    for part in range(2):
                        exps(0, 0, u, part)

            def head(b, g, hg, kind):
                T = t_base(hg)
                values(hg)
                half(hg * 2, T, 0, True, b + 1 if kind == "next batch" else None)
                if kind != "end":
                    keys(hg + 1, T + TV + TH)
                half(hg * 2 + 1, T + TV + TH, 1, kind != "end", None, done=3 if kind != "end" else 0)

            act.sem_inc(t_hi, TURN_CREDIT)
            over_heads(act, prologue, head)

        @block.vector
        def _(dve):
            def read_scores(n, t, k):
                u, c = divmod(k, NCH)
                start, _, width = KCH[c]
                dve.wait_ge(s_filled, n * SCH + k + 1)
                dve.sem_inc(dve_passed, 1)
                dve.tensor_tensor_reduce(out=probs[:, t, u, start:start + width], in0=s_bank[k % 2][:, 0:width],
                                         in1=mask_t[:, t, start:start + width], scale=1.0, scalar=NEG_HUGE,
                                         op0=ALU.add, op1=ALU.max, accum_out=chunk_max[:, t, u, c:c + 1]).then_inc(s_read, 1)
                if c == NCH - 1:
                    dve.wait_ge(s_read, n * SCH + k + 1 + READ_CREDIT)
                    dve.tensor_reduce(neg_max[:, t, u:u + 1], chunk_max[:, t, u, :], AX.X, ALU.max, negate=True).then_inc(max_done, 1)

            def context(b, q):
                c, start, real = piece(q)
                dve.wait_ge(ctx_hi, b * PIECES + q + 1)
                dve.tensor_tensor(out=ctxT_hl[:, 1, c, start:start + real], in0=ctx_raw[:, q % 2, 0:real],
                                  in1=ctxT_hl[:, 0, c, start:start + real].bitcast(F32), op=ALU.subtract).then_inc(ctx_lo, 1)

            def low(T, t, i):
                dve.wait_ge(t_hi, T + i + 1)
                bank, j = t_bank[i % RING], i - VOFF[t]
                if j < -1:
                    high, dst = v_hl[:, 0, 4 * i:4 * i + 4, :], v_hl[:, 1, 4 * i:4 * i + 4, :]
                    src = bank[:, :].rearrange("p (j d) -> p j d", d=DH)
                elif j == -1:
                    high, dst = (v_hl[0:KREM, h, KTILES - 1, :] for h in range(2))
                    src = bank[0:KREM, 0:DH]
                else:
                    high, dst = (pT_hl[0:key_rows(j), j % RING, h, :] for h in range(2))
                    src = bank[0:key_rows(j), :]
                dve.tensor_tensor(out=dst, in0=src, in1=high.bitcast(F32), op=ALU.subtract).then_inc(t_lo, 1)

            def half(n, T, t, more, hg, b, next_b, done=0):
                for i in range(done, 2):
                    low(T, t, i)
                if more:
                    dve.wait_ge(mask_in[1 - t], 16 * ((next_b if t == 1 and next_b is not None else b) + 1))
                for i in range(STEPS[t]):
                    if 2 <= i + 1 < STEPS[t]:
                        low(T, t, i + 1)
                    if more:
                        for k in chunks_at[t][i]:
                            read_scores(n + 1, 1 - t, k)
                    if t == 0 and next_b is not None and i < PIECES:
                        context(next_b, i)
                    if i == SUM_AT:
                        dve.wait_ge(exp_done, (n + 1) * HPG * 2)
                        dve.tensor_tensor(out=row_sum[:, :], in0=part_sum[:, t, :, 0], in1=part_sum[:, t, :, 1],
                                          op=ALU.add).then_inc(sum_done, 1)
                    if i == SUM_AT + 1:
                        dve.wait_ge(sum_done, n + 1)
                        dve.reciprocal(inv_sum[:, :], row_sum[:, :]).then_inc(inv_done, 1)
                dve.wait_ge(t_hi, T + STEPS[t] + 1)
                dve.wait_ge(pv_done, (n + 1) * KTILES)
                dve.wait_ge(o_stored[t], 16 * (hg + 1))
                dve.tensor_tensor(out=oT[:, t, :], in0=o_bank[:, :], in1=inv_rows[:, :], op=ALU.mult).then_inc(t_lo, 1)

            def keys(hg, T=None):
                for c, (start, width, _) in enumerate(KCH):
                    i = hg * NCH + c
                    if c == NCH - 1 and T is not None:
                        low(T, 1, 0)
                        low(T, 1, 1)
                    bank, r = p_bank[c % 2], c % 2
                    dve.wait_ge(p_filled, hg * 2 * NCH + c + 1)
                    if T is not None or c >= 2:
                        dve.wait_ge(k_lo, i - 1)
                    cols = slice(start, start + width)
                    dve.tensor_tensor(out=rot[0:64, r, 0:width], in0=bank[64:128, 0:width], in1=sin_t[64:128, cols], op=ALU.mult)
                    dve.tensor_tensor(out=rot[64:128, r, 0:width], in0=bank[0:64, 0:width], in1=sin_t[0:64, cols], op=ALU.mult)
                    dve.tensor_tensor(out=straight[:, r, 0:width], in0=bank[:, 0:width], in1=cos_t[:, cols], op=ALU.mult).then_inc(k_mul, 1)
                    dve.wait_ge(k_mul, i + 1)
                    dve.tensor_tensor(out=rot[:, r, 0:width], in0=rot[:, r, 0:width], in1=straight[:, r, 0:width],
                                      op=ALU.add).then_inc(k_sum, 1)

            def prologue():
                dve.sem_inc(s_read, READ_CREDIT)
                dve.sem_inc(t_lo, TURN_CREDIT)
                for q in range(PIECES):
                    context(0, q)
                dve.wait_ge(tab_in, 32)
                keys(0)
                dve.wait_ge(mask_in[0], 16)
                for k in range(SCH):
                    read_scores(0, 0, k)

            def head(b, g, hg, kind):
                T = t_base(hg)
                next_b = b + 1 if kind == "next batch" else None
                half(hg * 2, T, 0, True, hg, b, next_b)
                if kind != "end":
                    keys(hg + 1, T + TV + TH)
                half(hg * 2 + 1, T + TV + TH, 1, kind != "end", hg, b, next_b, done=2 if kind != "end" else 0)

            over_heads(dve, prologue, head)

        @block.tensor
        def _(pe):
            def project(w_hl, bank, start, width):
                steps = [(a, b, k) for a, b in PARTS for k in range(DC)]
                for a, b, k in steps:
                    last = pe.matmul(bank[:, 0:width], w_hl[:, a, k, :], ctxT_hl[:, b, k, start:start + width],
                                     start=(a, b, k) == steps[0], stop=(a, b, k) == steps[-1])
                last.then_inc(p_filled, 1)

            def keys(hg, b, T=None):
                pe.wait_ge(wk_lo, hg + 1)
                pe.wait_ge(ctx_lo, (b + 1) * PIECES)
                for c, (start, width, _) in enumerate(KCH):
                    if c == NCH - 1 and T is not None:
                        fill(hg * 2 - 1, T, 1, 0, hg - 1)
                        fill(hg * 2 - 1, T, 1, 1, hg - 1)
                    if c >= 2:
                        pe.wait_ge(k_mul, hg * NCH + c - 1)
                    project(wk_hl, p_bank[c % 2], start, width)

            def values(hg):
                pe.wait_ge(wv_lo, hg + 1)
                for c, (start, width, _) in enumerate(KCH):
                    if c < 2:
                        pe.wait_ge(k_mul, hg * NCH + c + 3)
                    else:
                        pe.wait_ge(vT_done, hg * NCH + c - 1)
                    project(wv_hl, p_bank[c % 2], start, width)

            def scores(n, t, k):
                u, c = divmod(k, NCH)
                start, width, _ = KCH[c]
                pe.wait_ge(s_read, n * SCH + k - 1 + READ_CREDIT)
                for i, (a, b) in enumerate(PARTS):
                    last = pe.matmul(s_bank[k % 2][:, 0:width], qT_hl[:, t, a, u * P:(u + 1) * P],
                                     kT_hl[:, b, start:start + width], start=i == 0, stop=i == 2)
                last.then_inc(s_filled, 1)

            def fill(n, T, t, i, hg):
                pe.wait_ge(t_lo, T + max(0, i - RING + 1))
                bank, j = t_bank[i % RING], i - VOFF[t]
                if j < 0:
                    tiles = range(4 * i, min(4 * i + 4, KTILES))
                    pe.wait_ge(vT_done, hg * NCH + sum(start < (tiles[-1] + 1) * P for start, _, _ in KCH))
                    for v in tiles:
                        rows = key_rows(v)
                        last = pe.transpose(bank[0:rows, (v % 4) * P:(v % 4 + 1) * P], vT[:, v * P:v * P + rows], ident[:, :])
                elif j < KTILES:
                    if j == 0:
                        pe.wait_ge(exp_done, (n + 1) * HPG * 2)
                    rows = key_rows(j)
                    for u in range(HPG):
                        last = pe.transpose(bank[0:rows, u * P:(u + 1) * P], probs[:, t, u, j * P:j * P + rows], ident[:, :])
                else:
                    pe.wait_ge(wide_done, n + 1)
                    for u in range(HPG):
                        last = pe.transpose(bank[:, u * P:(u + 1) * P], inv_wide[:, u, :], ident[:, :])
                last.then_inc(t_filled, 1)

            def half(n, T, t, more, hg, done=0):
                for i in range(done, 2):
                    fill(n, T, t, i, hg)
                for i in range(STEPS[t]):
                    if i + 2 <= STEPS[t]:
                        fill(n, T, t, i + 2, hg)
                    if more:
                        for k in chunks_at[t][i]:
                            if k == 0:
                                pe.wait_ge(q_in[1 - t], 16 * (hg + 1 + t))
                            if t == 1 and k < NCH:
                                pe.wait_ge(k_lo, (hg + 1) * NCH + k + 1)
                            scores(n + 1, 1 - t, k)
                    j = i - VOFF[t]
                    if j >= 0:
                        rows = key_rows(j)
                        pe.wait_ge(t_lo, T + i + 1)
                        for p, (a, b) in enumerate(PARTS):
                            last = pe.matmul(o_bank[:, :], v_hl[0:rows, a, j, :], pT_hl[0:rows, j % RING, b, :],
                                             start=j == 0 and p == 0, stop=j == KTILES - 1 and p == 2)
                        last.then_inc(pv_done, 1)

            def prologue():
                pe.sem_inc(t_filled, TURN_CREDIT)
                pe.wait_ge(ident_done, 1)
                pe.wait_ge(pad_set, 1)
                keys(0, 0)
                pe.wait_ge(q_in[0], 16)
                pe.wait_ge(k_lo, NCH)
                for k in range(SCH):
                    scores(0, 0, k)

            def head(b, g, hg, kind):
                T = t_base(hg)
                values(hg)
                half(hg * 2, T, 0, True, hg)
                if kind != "end":
                    keys(hg + 1, b + 1 if kind == "next batch" else b, T + TV + TH)
                half(hg * 2 + 1, T + TV + TH, 1, kind != "end", hg, done=2 if kind != "end" else 0)

            over_heads(pe, prologue, head)


def projection_stage(nc, sem, x, wo, o_scratch, x2):
    PAIRS = KVH // 2
    with ExitStack() as ctx:
        sb = lambda name, shape, dt=F32: ctx.enter_context(nc.sbuf_tensor(name, shape, dt))
        w_raw = sb("p_w_raw", [P, 2, HPG, DM])
        w_hl = sb("p_w_hl", [P, 2, 2, HPG, DM], F32R)
        o_raw = sb("p_o_raw", [P, 2, NT, HW])
        o_hl = sb("p_o_hl", [P, 2, 2, NT, HW], F32R)
        xt = sb("p_x", [P, NT, DM])
        acc = [ctx.enter_context(nc.psum_tensor(f"p_acc{n}", [P, DM], F32)) for n in range(NT)]
        x_in = sem("p_x_in")
        w_in = [sem(f"p_w_in{s}") for s in range(2)]
        o_in = [sem(f"p_o_in{s}") for s in range(2)]
        w_hi, w_lo, o_hi, o_lo = sem("p_w_hi"), sem("p_w_lo"), sem("p_o_hi"), sem("p_o_lo")
        group_done = sem("p_group_done")
        x2_done = sem("p_x2_done")
        GROUP_CREDIT = 2

        wo_v = wo.rearrange("(g h p) n -> g p h n", p=P, h=HPG)
        block = ctx.enter_context(nc.Block())

        @block.sync
        def _(sp):
            def load(group, s):
                sp.dma_start(w_raw[:, s, :, :], wo_v[bass.ds(group, 1), :, :, :].rearrange("o p h n -> (o p) h n")).then_inc(w_in[s], 16)
                sp.dma_start(o_raw[:, s, :, :], o_scratch[bass.ds(group, 1), :, :, :].rearrange("o n p w -> p (o n) w")).then_inc(o_in[s], 16)

            for s in range(2):
                load(s, s)
            sp.dma_start(xt[:, :, :], x.rearrange("b (t p) d -> p (b t) d", p=P)).then_inc(x_in, 16)
            with sp.Fori(0, PAIRS - 1) as pair:
                for s in range(2):
                    group = pair * 2 + s
                    sp.wait_ge(w_lo, group + 1)
                    sp.wait_ge(o_lo, group + 1)
                    load(group + 2, s)

        @block.scalar
        def _(act):
            with act.Fori(0, PAIRS) as pair:
                for s in range(2):
                    group = pair * 2 + s
                    act.wait_ge(group_done, group - 1 + GROUP_CREDIT)
                    act.wait_ge(w_in[s], 16 * (pair + 1))
                    act.activation(w_hl[:, s, 0, :, :], w_raw[:, s, :, :], ACT.Copy).then_inc(w_hi, 1)
                    act.wait_ge(o_in[s], 16 * (pair + 1))
                    act.activation(o_hl[:, s, 0, :, :], o_raw[:, s, :, :], ACT.Copy).then_inc(o_hi, 1)

        @block.gpsimd
        def _(pool):
            with pool.Fori(0, PAIRS) as pair:
                for s in range(2):
                    pool.wait_ge(w_hi, pair * 2 + s + 1)
                    pool.tensor_tensor(out=w_hl[:, s, 1, :, :], in0=w_raw[:, s, :, :],
                                       in1=w_hl[:, s, 0, :, :].bitcast(F32), op=ALU.subtract).then_inc(w_lo, 1)

        @block.vector
        def _(dve):
            with dve.Fori(0, PAIRS) as pair:
                for s in range(2):
                    dve.wait_ge(o_hi, pair * 2 + s + 1)
                    dve.tensor_tensor(out=o_hl[:, s, 1, :, :], in0=o_raw[:, s, :, :],
                                      in1=o_hl[:, s, 0, :, :].bitcast(F32), op=ALU.subtract).then_inc(o_lo, 1)
            dve.wait_ge(x_in, 16)
            dve.wait_ge(group_done, KVH + GROUP_CREDIT)
            for n in range(NT):
                dve.tensor_tensor(out=x2[:, n, :], in0=acc[n][:, :], in1=xt[:, n, :], op=ALU.add).then_inc(x2_done, 1)
            dve.wait_ge(x2_done, NT)

        @block.tensor
        def _(pe):
            pe.sem_inc(group_done, GROUP_CREDIT)

            def group(pair, s, first=False, final=False):
                pe.wait_ge(w_lo, pair * 2 + s + 1)
                pe.wait_ge(o_lo, pair * 2 + s + 1)
                for hh in range(HPG):
                    for n in range(NT):
                        for i, (a, b) in enumerate(PARTS):
                            last = pe.matmul(acc[n][:, :], o_hl[:, s, a, n, hh * P:(hh + 1) * P], w_hl[:, s, b, hh, :],
                                             start=first and hh == 0 and i == 0, stop=final and hh == HPG - 1 and i == 2)
                last.then_inc(group_done, 1)

            group(0, 0, first=True)
            group(0, 1)
            with pe.Fori(1, PAIRS - 1) as pair:
                for s in range(2):
                    group(pair, s)
            group(PAIRS - 1, 0)
            group(PAIRS - 1, 1, final=True)


def dense_stage(nc, sem, kern, bias, gate_t, lora_a, lora_b_t, a_shared_t, b_shared_t, x2, out):
    NK = LORAS * RANK // P
    APK = P // RANK
    with ExitStack() as ctx:
        sb = lambda name, shape, dt=F32: ctx.enter_context(nc.sbuf_tensor(name, shape, dt))
        ident = sb("d_ident", [P, P])
        diag = sb("d_diag", [P, RANK])
        k_raw = sb("d_k_raw", [P, DC, DM])
        k_hl = sb("d_k_hl", [P, 2, DC, DM], F32R)
        bias_rows = sb("d_bias", [P, DM])
        x2_bias = sb("d_x2_bias", [P, NT, DM])
        a_raw = sb("d_a_raw", [P, NK, DM])
        asT_raw = sb("d_asT_raw", [P, DC, RANK])
        bsT_raw = sb("d_bsT_raw", [RANK, DM])
        gates = sb("d_gates", [P, NK, NT])
        G = sb("d_G", [P, NK, NT, RANK])
        bT = sb("d_bT", [P, NK, DM])
        asT_hl = sb("d_asT_hl", [P, 2, DC, RANK], F32R)
        bs_hl = sb("d_bs_hl", [RANK, 2, DM], F32R)
        aT_hl = sb("d_aT_hl", [P, 2, DC, NT * RANK], F32R)
        b_hl = sb("d_b_hl", [P, 2, 2, DM], F32R)
        stats = sb("d_stats", [P, NT, 6])
        mean_var = sb("d_mean_var", [P, NT, 2])
        var_eps = sb("d_var_eps", [P, NT])
        minus_half = sb("d_minus_half", [P, NT])
        rstd = sb("d_rstd", [P, NT])
        xn = sb("d_norm", [P, NT, DM])
        xT_hl = sb("d_xT_hl", [P, 2, DC, NT * P], F32R)
        ax_hl = sb("d_ax_hl", [P, 2, NT, P], F32R)
        axs_hl = sb("d_axs_hl", [RANK, 2, NT * P], F32R)
        y = sb("d_y", [P, NT, DM])
        bank = [ctx.enter_context(nc.psum_tensor(f"d_b{i}", [P, DM], F32)) for i in range(4)]
        y_bank = [ctx.enter_context(nc.psum_tensor(f"d_y{i}", [P, DM], F32)) for i in range(4)]

        lora_in, gates_in = sem("d_lora_in"), sem("d_gates_in")
        k_in, bias_in = sem("d_k_in"), sem("d_bias_in")
        ident_set, ident_done, half_set, zeroed = sem("d_ident_set"), sem("d_ident_done"), sem("d_half_set"), sem("d_zeroed")
        diag_done, G_done = sem("d_diag_done"), sem("d_G_done")
        k_hi, k_lo, xb_done = sem("d_k_hi"), sem("d_k_lo"), sem("d_xb_done")
        stat_done, aggr_done, veps_done = sem("d_stat_done"), sem("d_aggr_done"), sem("d_veps_done")
        rstd_done, xn_done = sem("d_rstd_done"), sem("d_xn_done")
        shared_hi, shared_lo = sem("d_shared_hi"), sem("d_shared_lo")
        filled, hi, lo = sem("d_filled"), sem("d_hi"), sem("d_lo")
        y_filled, y_done, stored = sem("d_y_filled"), sem("d_y_done"), sem("d_stored")

        F_AT, F_B, F_XT, F_AX, F_AXS = 0, 2, 4, 12, 14

        block = ctx.enter_context(nc.Block())

        @block.sync
        def _(sp):
            for n in range(APK):
                sp.dma_start(gates[n * RANK:(n + 1) * RANK, :, :],
                             gate_t.rearrange("(k n) b -> n k b", n=APK)[n:n + 1, :, :].to_broadcast([RANK, NK, NT])
                             ).then_inc(gates_in, 16)
            sp.dma_start(bT[:, :, :], lora_b_t.rearrange("n r o -> (n r) o").rearrange("(k p) o -> p k o", p=P)).then_inc(lora_in, 16)
            sp.dma_start(a_raw[:, :, :], lora_a.rearrange("n r i -> (n r) i").rearrange("(k p) i -> p k i", p=P)).then_inc(lora_in, 16)
            sp.dma_start(asT_raw[:, :, :], a_shared_t.rearrange("(c p) r -> p c r", p=P)).then_inc(lora_in, 16)
            sp.dma_start(bsT_raw[:, :], b_shared_t).then_inc(lora_in, 16)
            sp.dma_start(k_raw[:, :, :], kern.rearrange("(c p) n -> p c n", p=P)).then_inc(k_in, 16)
            sp.dma_start(bias_rows[:, :], bias.rearrange("(o n) -> o n", o=1).to_broadcast([P, DM])).then_inc(bias_in, 16)
            out_v = out.rearrange("b (t p) d -> (b t) p d", p=P)
            for n in range(NT):
                sp.wait_ge(y_done, n + 1)
                sp.dma_start(out_v[n, :, :], y[:, n, :]).then_inc(stored, 16)
            sp.wait_ge(stored, 16 * NT)

        @block.gpsimd
        def _(pool):
            pool.memset(ident[:, :], 0.0).then_inc(ident_set, 1)
            pool.memset(minus_half[:, :], -0.5).then_inc(half_set, 1)
            pool.wait_ge(ident_set, 1)
            pool.affine_select(out=ident[:, :], in_=ident[:, :], compare_op=ALU.not_equal, fill=1.0,
                               base=0, pattern=[[-1, P]], channel_multiplier=1).then_inc(ident_done, 1)
            pool.memset(ax_hl[:, :, :, :].bitcast(F32), 0.0).then_inc(zeroed, 1)
            pool.wait_ge(half_set, 1)
            pool.wait_ge(veps_done, 1)
            pool.tensor_tensor(out=rstd[:, :], in0=var_eps[:, :], in1=minus_half[:, :], op=ALU.pow).then_inc(rstd_done, 1)
            pool.wait_ge(k_hi, 1)
            pool.tensor_tensor(out=k_hl[:, 1, :, :], in0=k_raw[:, :, :], in1=k_hl[:, 0, :, :].bitcast(F32), op=ALU.subtract).then_inc(k_lo, 1)
            pool.wait_ge(bias_in, 16)
            for n in range(NT):
                pool.tensor_tensor(out=x2_bias[:, n, :], in0=x2[:, n, :], in1=bias_rows[:, :], op=ALU.add).then_inc(xb_done, 1)

        def drains():
            for i in range(2):
                yield F_AT + i, bank[(F_AT + i) % 4][:, :].rearrange("p (c m) -> p c m", c=2), [aT_hl[:, h, 2 * i:2 * i + 2, :] for h in range(2)]
            for i in range(2):
                yield F_B + i, bank[(F_B + i) % 4][:, :], [b_hl[:, h, i, :] for h in range(2)]
            for n in range(NT):
                yield F_XT + n, bank[(F_XT + n) % 4][:, :].rearrange("p (c q) -> p c q", q=P), [xT_hl[:, h, :, n * P:(n + 1) * P] for h in range(2)]
            for i in range(2):
                for q in range(APK):
                    rows = slice(q * RANK, (q + 1) * RANK)
                    yield F_AX + i, bank[(F_AX + i) % 4][rows, q * P:(q + 1) * P], [ax_hl[rows, h, 4 * i + q, :] for h in range(2)]
            for i in range(2):
                yield F_AXS + i, bank[(F_AXS + i) % 4][0:RANK, :], [axs_hl[:, h, 512 * i:512 * (i + 1)] for h in range(2)]

        @block.scalar
        def _(act):
            act.wait_ge(k_in, 16)
            act.activation(k_hl[:, 0, :, :], k_raw[:, :, :], ACT.Copy).then_inc(k_hi, 1)
            act.wait_ge(lora_in, 16 * 4)
            act.activation(asT_hl[:, 0, :, :], asT_raw[:, :, :], ACT.Copy).then_inc(shared_hi, 1)
            act.activation(bs_hl[:, 0, :], bsT_raw[:, :], ACT.Copy).then_inc(shared_hi, 1)
            act.wait_ge(zeroed, 1)
            for f, src, (high, _) in drains():
                act.wait_ge(filled, f + 1)
                act.activation(high, src, ACT.Copy).then_inc(hi, 1)

        @block.vector
        def _(dve):
            for n in range(NT):
                dve.bn_stats(stats[:, n, :], x2[:, n, :]).then_inc(stat_done, 1)
            for n in range(NT):
                dve.wait_ge(stat_done, n + 1)
                dve.bn_aggr(mean_var[:, n, :], stats[:, n, :]).then_inc(aggr_done, 1)
            dve.wait_ge(aggr_done, NT)
            dve.tensor_scalar(var_eps[:, :], mean_var[:, :, 1], EPS, None, ALU.add).then_inc(veps_done, 1)
            dve.wait_ge(ident_done, 1)
            for n in range(APK):
                rows = slice(n * RANK, (n + 1) * RANK)
                dve.tensor_copy(diag[rows, :], ident[rows, rows]).then_inc(diag_done, 1)
            dve.wait_ge(diag_done, APK)
            dve.wait_ge(gates_in, 16 * APK)
            dve.tensor_tensor(out=G[:, :, :, :].rearrange("p k b r -> p (k b) r"),
                              in0=gates[:, :, :].rearrange("p k b -> p (k b)").unsqueeze(2).to_broadcast([P, NK * NT, RANK]),
                              in1=diag[:, :].unsqueeze(1).to_broadcast([P, NK * NT, RANK]), op=ALU.mult).then_inc(G_done, 1)
            dve.wait_ge(shared_hi, 2)
            dve.tensor_tensor(out=asT_hl[:, 1, :, :], in0=asT_raw[:, :, :], in1=asT_hl[:, 0, :, :].bitcast(F32), op=ALU.subtract).then_inc(shared_lo, 1)
            dve.tensor_tensor(out=bs_hl[:, 1, :], in0=bsT_raw[:, :], in1=bs_hl[:, 0, :].bitcast(F32), op=ALU.subtract).then_inc(shared_lo, 1)
            dve.wait_ge(rstd_done, 1)
            for n in range(NT):
                dve.tensor_scalar(xn[:, n, :], x2[:, n, :], mean_var[:, n, 0:1], rstd[:, n:n + 1],
                                  ALU.subtract, ALU.mult).then_inc(xn_done, 1)
            for i, (f, src, (high, low)) in enumerate(drains()):
                dve.wait_ge(hi, i + 1)
                ins = dve.tensor_tensor(out=low, in0=src, in1=high.bitcast(F32), op=ALU.subtract)
                if f not in (F_AX, F_AX + 1) or (i - F_AX) % APK == APK - 1:
                    ins.then_inc(lo, 1)
            for n in range(NT):
                dve.wait_ge(y_filled, n + 1)
                dve.wait_ge(xb_done, n + 1)
                dve.tensor_tensor(out=y[:, n, :], in0=y_bank[n % 4][:, :], in1=x2_bias[:, n, :], op=ALU.add).then_inc(y_done, 1)

        @block.tensor
        def _(pe):
            def free(f):
                if f >= 4:
                    pe.wait_ge(lo, f - 3)

            def three(dst, stationary, moving, start=True, stop=True):
                for i, (a, b) in enumerate(PARTS):
                    last = pe.matmul(dst, stationary(a), moving(b), start=start and i == 0, stop=stop and i == 2)
                return last

            pe.wait_ge(ident_done, 1)
            pe.wait_ge(lora_in, 16 * 4)
            pe.wait_ge(G_done, 1)
            for i in range(2):
                free(F_AT + i)
                for cc in range(2):
                    c = 2 * i + cc
                    for k in range(NK):
                        last = pe.matmul(bank[(F_AT + i) % 4][:, cc * 256:(cc + 1) * 256], a_raw[:, k, c * P:(c + 1) * P],
                                         G[:, k, :, :].rearrange("p b r -> p (b r)"), start=k == 0, stop=k == NK - 1)
                last.then_inc(filled, 1)
            for i in range(2):
                free(F_B + i)
                for k in range(NK):
                    last = pe.matmul(bank[(F_B + i) % 4][:, :], G[:, k, i * APK:(i + 1) * APK, :].rearrange("p b r -> p (b r)"),
                                     bT[:, k, :], start=k == 0, stop=k == NK - 1)
                last.then_inc(filled, 1)
            for n in range(NT):
                pe.wait_ge(xn_done, n + 1)
                free(F_XT + n)
                for c in range(DC):
                    last = pe.transpose(bank[(F_XT + n) % 4][:, c * P:(c + 1) * P], xn[:, n, c * P:(c + 1) * P], ident[:, :])
                last.then_inc(filled, 1)
            for i in range(2):
                pe.wait_ge(lo, F_XT + 4 * i + 4)
                free(F_AX + i)
                for c in range(DC):
                    last = three(bank[(F_AX + i) % 4][:, :], lambda h: aT_hl[:, h, c, i * P:(i + 1) * P],
                                 lambda h: xT_hl[:, h, c, 512 * i:512 * (i + 1)], start=c == 0, stop=c == DC - 1)
                last.then_inc(filled, 1)
            for i in range(2):
                free(F_AXS + i)
                for c in range(DC):
                    last = three(bank[(F_AXS + i) % 4][0:RANK, :], lambda h: asT_hl[:, h, c, :],
                                 lambda h: xT_hl[:, h, c, 512 * i:512 * (i + 1)], start=c == 0, stop=c == DC - 1)
                last.then_inc(filled, 1)
            pe.wait_ge(k_lo, 1)
            pe.wait_ge(shared_lo, 2)
            for n in range(NT):
                if n >= 4:
                    pe.wait_ge(y_done, n - 3)
                if n == 0:
                    pe.wait_ge(lo, F_AXS + 1)
                if n == 4:
                    pe.wait_ge(lo, F_AXS + 2)
                tile = slice(n * P, (n + 1) * P)
                for c in range(DC):
                    three(y_bank[n % 4][:, :], lambda h: xT_hl[:, h, c, tile], lambda h: k_hl[:, h, c, :], start=c == 0, stop=False)
                three(y_bank[n % 4][:, :], lambda h: ax_hl[:, h, n, :], lambda h: b_hl[:, h, n // 4, :], start=False, stop=False)
                last = three(y_bank[n % 4][:, :], lambda h: axs_hl[:, h, tile], lambda h: bs_hl[:, h, :], start=False)
                last.then_inc(y_filled, 1)


def program(nc, x, ctx_t, mask, wq, wk, wv, wo, gate_t, kern, bias, lora_a, lora_b_t, a_shared_t, b_shared_t,
            cos_q, sin_q, cos_k, sin_k, out):
    with ExitStack() as ctx:
        sem = lambda name: ctx.enter_context(nc.semaphore(name))
        q_scratch = nc.dram_tensor("q_scratch", (KVH, NT, P, 2 * HW), F32R, kind="Internal").ap()
        o_scratch = nc.dram_tensor("o_scratch", (KVH, NT, P, HW), F32, kind="Internal").ap()
        query_stage(nc, sem, x, wq, cos_q, sin_q, q_scratch)
        attention_stage(nc, sem, ctx_t, mask, wk, wv, cos_k, sin_k, q_scratch, o_scratch)
        x2 = ctx.enter_context(nc.sbuf_tensor("x2", [P, NT, DM], F32))
        projection_stage(nc, sem, x, wo, o_scratch, x2)
        dense_stage(nc, sem, kern, bias, gate_t, lora_a, lora_b_t, a_shared_t, b_shared_t, x2, out)


def rotary_tables(np):
    f = np.float32
    inv_freq = f(1.0) / np.power(f(10000.0), np.arange(0, DH, 2, dtype=f) / f(DH))
    angle = np.arange(SKP, dtype=f)[None, :] * inv_freq[:, None]
    cos, sin = np.cos(angle.astype(np.float64)), np.sin(angle.astype(np.float64))
    cos, sin = np.concatenate([cos, cos]), np.concatenate([sin, -sin])
    scale = 1.0 / np.sqrt(float(DH))
    q = lambda a: np.tile(a[:, :SQ] * scale, (1, 512 // SQ)).astype(f)
    return q(cos), q(sin), cos.astype(f), sin.astype(f)


_INS = ["x", "ctx_4096", "mask_BxSxS2_ff0", "L0_xattn_wq", "L0_xattn_wk", "L0_xattn_wv", "L0_xattn_wo",
        "L0_ffn_gate", "L0_ffn_kernel", "L0_ffn_bias", "L0_ffn_lora_A", "L0_ffn_lora_B",
        "L0_ffn_lora_A_shared", "L0_ffn_lora_B_shared"]
_TABLES = ["cos_q", "sin_q", "cos_k", "sin_k"]


def kernel(**inputs):
    import numpy as np
    import concourse.bacc as bacc
    from concourse.bass_utils import run_bass_kernel_spmd

    nc = bacc.Bacc("TRN2", target_bir_lowering=False, num_devices=1)
    arrays, args = {}, []
    lay = {"ctx_4096": (0, 2, 1), "L0_ffn_gate": (1, 0), "L0_ffn_lora_B": (0, 2, 1), "L0_ffn_lora_A_shared": (1, 0), "L0_ffn_lora_B_shared": (1, 0)}
    named = [(n, np.ascontiguousarray(np.transpose(inputs[n], lay.get(n, range(np.ndim(inputs[n])))))) for n in _INS] + list(zip(_TABLES, rotary_tables(np)))
    for name, a in named:
        arrays[f"in_{name}"] = a
        args.append(nc.dram_tensor(f"in_{name}", a.shape, mybir.dt.from_np(a.dtype), kind="ExternalInput").ap())
    args.append(nc.dram_tensor("out", (BATCH, SQ, DM), F32, kind="ExternalOutput").ap())
    program(nc, *args)
    r = run_bass_kernel_spmd(nc, [arrays], core_ids=[0])
    return r.results[0]["out"]
```

```python
from contextlib import ExitStack

import concourse.bass as bass
import concourse.mybir as mybir
from concourse.alu_op_type import AluOpType as ALU

F32 = mybir.dt.float32
F32R = mybir.dt.float32r
ACT = mybir.ActivationFunctionType
AX = mybir.AxisListType

P = 128
BATCH, SQ, DM = 4, 256, 512
SK = 1601
HEADS, KVH, DH = 32, 8, 128
HPG = HEADS // KVH
DC = DM // P
QT = SQ // P
NT = BATCH * QT
HW = HPG * P
SKP = SK + 1
KTILES = -(-SK // P)
KREM = SK - (KTILES - 1) * P
KCH = [(0, 402, 402), (402, 400, 400), (802, 400, 400), (1202, 400, 399)]
NCH = len(KCH)
SCH = HPG * NCH
PARTS = [(0, 0), (0, 1), (1, 0)]
RING = 3
TV, TH = -(-KTILES // 4), KTILES
TG = TV + 2 * TH
Q_LAST = 16 * (KVH // 2 + 2 * HPG)
LORAS, RANK = 16, 32
NK = LORAS * RANK // P
APK = P // RANK
EPS = 1e-5
NEG_HUGE = -3.4e38


def key_rows(j):
    return KREM if j == KTILES - 1 else P


def query_stage(nc, sem, x, wq, cos_q, sin_q, q_scratch, ctx_t, wk, ctx_first, wk_first, ctx_first_in, wk_first_in,
                q_stored):
    ROT = 4
    CH = HPG * NT // 4
    PAIRS = KVH // 2
    with ExitStack() as ctx:
        sb = lambda name, shape, dt=F32: ctx.enter_context(nc.sbuf_tensor(name, shape, dt))
        ps = lambda name: ctx.enter_context(nc.psum_tensor(name, [P, 512], F32))
        ident = sb("q_ident", [P, P])
        xt = sb("q_x", [P, NT, DM])
        stats = sb("q_stats", [P, NT, 6])
        mean_var = sb("q_mean_var", [P, NT, 2])
        var_eps = sb("q_var_eps", [P, NT])
        minus_half = sb("q_minus_half", [P, NT])
        rstd = sb("q_rstd", [P, NT])
        cos_t = sb("q_cos", [P, 512])
        sin_t = sb("q_sin", [P, 512])
        xT_hl = sb("q_xT_hl", [P, 2, DC, NT * P], F32R)
        w_raw = sb("q_w_raw", [P, 2, DC, HW])
        w_hl = sb("q_w_hl", [P, 2, 2, DC, HW], F32R)
        rot = sb("q_rot", [P, ROT, 512])
        straight = sb("q_straight", [P, 2, 512])
        q_out = sb("q_out", [P, 2, NT, 2, HW], F32R)
        t_bank = [ps(f"q_t{i}") for i in range(2)]
        q_bank = [ps(f"q_q{i}") for i in range(4)]
        t_bank += q_bank[1:]

        x_in = [sem(f"q_x_in{i}") for i in range(NT // 2)]
        tab_in = sem("q_tab_in")
        w_in = [sem(f"q_w_in{i}") for i in range(2)]
        ident_set, ident_done, half_set = sem("q_ident_set"), sem("q_ident_done"), sem("q_half_set")
        stat_done, aggr_done, veps_done = sem("q_stat_done"), sem("q_aggr_done"), sem("q_veps_done")
        rstd_done, xn_done = sem("q_rstd_done"), sem("q_xn_done")
        t_filled, t_hi, t_lo = sem("q_t_filled"), sem("q_t_hi"), sem("q_t_lo")
        w_hi, w_lo = sem("q_w_hi"), sem("q_w_lo")
        q_filled, q_mul, q_sum = sem("q_q_filled"), sem("q_q_mul"), sem("q_q_sum")
        q_hi, q_lo = sem("q_q_hi"), sem("q_q_lo")

        PARTS_OF_X = [slice(0, NT // 2), slice(NT // 2, NT)]
        wq_v = wq.rearrange("(c p) n -> p c n", p=P)
        MUL_CREDIT, LO_CREDIT, FILLED_CREDIT = len(q_bank), ROT, 2 * CH
        block = ctx.enter_context(nc.Block())

        @block.sync
        def _(sp):
            for i in range(NT // 2):
                sp.dma_start(xt[:, 2 * i:2 * i + 2, :], x.rearrange("b (t p) d -> p (b t) d", p=P)[:, 2 * i:2 * i + 2, :]
                             ).then_inc(x_in[i], 16)
            sp.dma_start(w_raw[:, 0, :, :], wq_v[:, :, 0:HW]).then_inc(w_in[0], 16)
            sp.dma_start(cos_t[:, :], cos_q).then_inc(tab_in, 16)
            sp.dma_start(sin_t[:, :], sin_q).then_inc(tab_in, 16)
            sp.dma_start(w_raw[:, 1, :, :], wq_v[:, :, HW:2 * HW]).then_inc(w_in[1], 16)
            for start, _, real in KCH:
                sp.dma_start(ctx_first[:, :, start:start + real],
                             ctx_t[0:1, :, start:start + real].rearrange("o (c p) k -> p (o c) k", p=P)).then_inc(ctx_first_in, 16)
            sp.dma_start(wk_first[:, :, :], wk.rearrange("(c p) n -> p c n", p=P)[:, :, 0:DH]).then_inc(wk_first_in, 16)

            def store(group, s):
                sp.wait_ge(q_lo, (group + 1) * CH + LO_CREDIT)
                sp.dma_start(q_scratch[bass.ds(group, 1), :, :, :].rearrange("o n p w -> p (o n) w").bitcast(F32),
                             q_out[:, s, :, :, :].rearrange("p n h w -> p n (h w)").bitcast(F32)).then_inc(q_stored[s], 16)

            with sp.Fori(0, PAIRS - 1) as pair:
                for s in range(2):
                    group = pair * 2 + s
                    sp.wait_ge(w_lo, (group + 1) * DC)
                    sp.dma_start(w_raw[:, s, :, :], wq_v[:, :, bass.ds((group + 2) * HW, HW)]).then_inc(w_in[s], 16)
                    store(group, s)
            store(KVH - 2, 0)
            for hh in range(HPG):
                sp.wait_ge(q_lo, (KVH - 1) * CH + 2 * hh + 2 + LO_CREDIT)
                for h in range(2):
                    cols = slice(h * HW + hh * P, h * HW + (hh + 1) * P)
                    sp.dma_start(q_scratch[KVH - 1, :, :, cols].rearrange("n p q -> p n q").bitcast(F32),
                                 q_out[:, 1, :, h, hh * P:(hh + 1) * P].bitcast(F32)).then_inc(q_stored[1], 16)
            sp.wait_ge(q_stored[0], 16 * (PAIRS + 1))
            sp.wait_ge(ctx_first_in, 16 * NCH)
            sp.wait_ge(wk_first_in, 16)

        @block.gpsimd
        def _(pool):
            pool.memset(ident[:, :], 0.0).then_inc(ident_set, 1)
            pool.memset(minus_half[:, :], -0.5).then_inc(half_set, 1)
            pool.sem_inc(q_lo, LO_CREDIT)
            pool.wait_ge(ident_set, 1)
            pool.affine_select(out=ident[:, :], in_=ident[:, :], compare_op=ALU.not_equal, fill=1.0,
                               base=0, pattern=[[-1, P]], channel_multiplier=1).then_inc(ident_done, 1)
            pool.wait_ge(half_set, 1)

            def weights_lo(group, s, k):
                pool.wait_ge(w_hi, group + 1)
                pool.tensor_tensor(out=w_hl[:, s, 1, k, :], in0=w_raw[:, s, k, :],
                                   in1=w_hl[:, s, 0, k, :].bitcast(F32), op=ALU.subtract).then_inc(w_lo, 1)

            def queries_lo(group, s, last=False):
                for c in range(CH):
                    hh, tc = divmod(c, 2)
                    if 2 <= c < 2 + DC and not last:
                        weights_lo(group + 1, 1 - s, c - 2)
                    pool.wait_ge(q_hi, group * CH + c + 1)
                    pool.tensor_tensor(
                        out=q_out[:, s, tc * 4:tc * 4 + 4, 1, hh * P:(hh + 1) * P],
                        in0=rot[:, c % ROT, :].rearrange("p (n q) -> p n q", q=P),
                        in1=q_out[:, s, tc * 4:tc * 4 + 4, 0, hh * P:(hh + 1) * P].bitcast(F32),
                        op=ALU.subtract).then_inc(q_lo, 1)

            for part, tiles in enumerate(PARTS_OF_X):
                pool.wait_ge(veps_done, part + 1)
                pool.tensor_tensor(out=rstd[:, tiles], in0=var_eps[:, tiles], in1=minus_half[:, tiles], op=ALU.pow).then_inc(rstd_done, 1)
            for k in range(DC):
                weights_lo(0, 0, k)
            with pool.Fori(0, PAIRS - 1) as pair:
                for s in range(2):
                    queries_lo(pair * 2 + s, s)
            queries_lo(KVH - 2, 0)
            queries_lo(KVH - 1, 1, last=True)

        @block.scalar
        def _(act):
            for s in range(2):
                act.sem_inc(q_stored[s], 16)

            def weights_hi(group, s, turn):
                act.wait_ge(w_in[s], 16 * (turn + 1))
                act.wait_ge(q_filled, (group - 1) * CH + FILLED_CREDIT)
                act.activation(w_hl[:, s, 0, :, :], w_raw[:, s, :, :], ACT.Copy).then_inc(w_hi, 1)

            def queries_hi(pair, s, last=False):
                group = pair * 2 + s
                act.wait_ge(q_stored[s], 16 * (pair + 1))
                for c in range(CH):
                    hh, tc = divmod(c, 2)
                    if c == 1 and not last:
                        weights_hi(group + 1, 1 - s, pair + s)
                    act.wait_ge(q_sum, group * CH + c + 1)
                    act.activation(q_out[:, s, tc * 4:tc * 4 + 4, 0, hh * P:(hh + 1) * P],
                                   rot[:, c % ROT, :].rearrange("p (n q) -> p n q", q=P), ACT.Copy).then_inc(q_hi, 1)

            for n in range(NT):
                if n == 2:
                    weights_hi(0, 0, 0)
                act.wait_ge(t_filled, n + 1)
                act.activation(xT_hl[:, 0, :, n * P:(n + 1) * P],
                               t_bank[n % len(t_bank)][:, :].rearrange("p (c q) -> p c q", q=P), ACT.Copy).then_inc(t_hi, 1)
            with act.Fori(0, PAIRS - 1) as pair:
                for s in range(2):
                    queries_hi(pair, s)
            queries_hi(PAIRS - 1, 0)
            queries_hi(PAIRS - 1, 1, last=True)

        @block.vector
        def _(dve):
            dve.sem_inc(q_mul, MUL_CREDIT)
            def tile_statistics(tiles):
                for n in tiles:
                    if n % 2 == 0:
                        dve.wait_ge(x_in[n // 2], 16)
                    dve.bn_stats(stats[:, n, :], xt[:, n, :]).then_inc(stat_done, 1)

            def part_statistics(part):
                tiles = PARTS_OF_X[part]
                for n in range(tiles.start, tiles.stop):
                    dve.wait_ge(stat_done, n + 1)
                    dve.bn_aggr(mean_var[:, n, :], stats[:, n, :]).then_inc(aggr_done, 1)
                dve.wait_ge(aggr_done, tiles.stop)
                dve.tensor_scalar(var_eps[:, tiles], mean_var[:, tiles, 1], EPS, None, ALU.add).then_inc(veps_done, 1)

            def normalise(part):
                dve.wait_ge(rstd_done, part + 1)
                for n in range(PARTS_OF_X[part].start, PARTS_OF_X[part].stop):
                    dve.tensor_scalar(xt[:, n, :], xt[:, n, :], mean_var[:, n, 0:1], rstd[:, n:n + 1],
                                      ALU.subtract, ALU.mult).then_inc(xn_done, 1)

            def transposed_lo(tiles):
                for n in tiles:
                    dve.wait_ge(t_hi, n + 1)
                    dve.tensor_tensor(out=xT_hl[:, 1, :, n * P:(n + 1) * P],
                                      in0=t_bank[n % len(t_bank)][:, :].rearrange("p (c q) -> p c q", q=P),
                                      in1=xT_hl[:, 0, :, n * P:(n + 1) * P].bitcast(F32),
                                      op=ALU.subtract).then_inc(t_lo, 1)

            tile_statistics(range(0, NT // 2))
            part_statistics(0)
            tile_statistics(range(NT // 2, NT // 2 + 2))
            normalise(0)
            tile_statistics(range(NT // 2 + 2, NT))
            part_statistics(1)
            transposed_lo(range(0, 2))
            normalise(1)
            transposed_lo(range(2, NT))
            dve.wait_ge(tab_in, 32)
            with dve.Fori(0, PAIRS) as pair:
                for s in range(2):
                    for c in range(CH):
                        i = (pair * 2 + s) * CH + c
                        bank, r = q_bank[c % 4], c % ROT
                        dve.wait_ge(q_filled, i + 1 + FILLED_CREDIT)
                        dve.wait_ge(q_lo, i + 1)
                        dve.tensor_tensor(out=rot[0:64, r, :], in0=bank[64:128, :], in1=sin_t[64:128, :], op=ALU.mult)
                        dve.tensor_tensor(out=rot[64:128, r, :], in0=bank[0:64, :], in1=sin_t[0:64, :], op=ALU.mult)
                        dve.tensor_tensor(out=straight[:, c % 2, :], in0=bank[:, :], in1=cos_t[:, :], op=ALU.mult).then_inc(q_mul, 1)
                        dve.wait_ge(q_mul, i + 1 + MUL_CREDIT)
                        dve.tensor_tensor(out=rot[:, r, :], in0=rot[:, r, :], in1=straight[:, c % 2, :], op=ALU.add).then_inc(q_sum, 1)

        @block.tensor
        def _(pe):
            def products(group, s):
                pe.wait_ge(w_hi, group + 1)
                for c in range(CH):
                    hh, tc = divmod(c, 2)
                    bank = q_bank[c % 4]
                    if c < 2:
                        pe.wait_ge(t_lo, PARTS_OF_X[c].stop)
                    pe.wait_ge(q_mul, group * CH + c - 3 + MUL_CREDIT)
                    steps = [(a, b, k) for a, b in PARTS for k in range(DC)]
                    for a, b, k in steps:
                        if c == 0 and (a, k) == (1, 0):
                            pe.wait_ge(w_lo, (group + 1) * DC)
                        last = pe.matmul(bank[:, :], w_hl[:, s, a, k, hh * P:(hh + 1) * P],
                                         xT_hl[:, b, k, tc * 512:(tc + 1) * 512],
                                         start=(a, b, k) == steps[0], stop=(a, b, k) == steps[-1])
                    last.then_inc(q_filled, 1)

            pe.sem_inc(q_filled, FILLED_CREDIT)
            pe.wait_ge(ident_done, 1)
            for n in range(NT):
                pe.wait_ge(xn_done, n + 1)
                if n >= len(t_bank):
                    pe.wait_ge(t_lo, n - len(t_bank) + 1)
                for c in range(DC):
                    last = pe.transpose(t_bank[n % len(t_bank)][:, c * P:(c + 1) * P], xt[:, n, c * P:(c + 1) * P], ident[:, :])
                last.then_inc(t_filled, 1)
            with pe.Fori(0, PAIRS) as pair:
                for s in range(2):
                    products(pair * 2 + s, s)


def attention_stage(nc, sem, ctx_t, mask, wk, wv, cos_k, sin_k, q_scratch, o_scratch, probs_1, w_raw, ctx_first_in, w_in,
                    last_q_stored, tables, gate_t, lora_a, gates, a_raw, gates_in, a_in):
    CTX_SLOTS = 4
    with ExitStack() as ctx:
        sb = lambda name, shape, dt=F32: ctx.enter_context(nc.sbuf_tensor(name, shape, dt))
        ps = lambda name: ctx.enter_context(nc.psum_tensor(name, [P, 512], F32))
        ident = sb("a_ident", [P, P])
        cos_t, sin_t = tables[:, 0, :], tables[:, 1, :]
        ctx_raw = sb("a_ctx_raw", [P, CTX_SLOTS, KCH[0][1]])
        ctxT_hl = sb("a_ctxT_hl", [P, 2, DC, SKP], F32R)
        mask_t = sb("a_mask", [P, QT, SK])
        wk_hl = sb("a_wk_hl", [P, 2, DC, DH], F32R)
        wv_hl = sb("a_wv_hl", [P, 2, DC, DH], F32R)
        vT = sb("a_vT", [P, SKP])
        v_hl = sb("a_v_hl", [P, 2, KTILES, DH], F32R)
        rot = sb("a_rot", [P, 2, KCH[0][1]])
        straight = sb("a_straight", [P, 2, KCH[0][1]])
        kT_hl = sb("a_kT_hl", [P, 2, SKP], F32R)
        ctx_first = probs_1
        pT_hl = sb("a_pT_hl", [P, RING, 2, HW], F32R)
        chunk_max = sb("a_chunk_max", [P, QT, HPG, NCH])
        neg_max = sb("a_neg_max", [P, QT, HPG])
        part_sum = sb("a_part_sum", [P, QT, HPG, 2])
        row_sum = sb("a_row_sum", [P, HPG])
        inv_sum = sb("a_inv_sum", [P, HPG])
        qT_hl = sb("a_qT_hl", [P, QT, 2, HW], F32R)
        probs = [sb("a_probs_0", [P, HPG, SK]), probs_1]
        inv_rows = sb("a_inv_rows", [P, HPG, P])
        oT = sb("a_oT", [P, QT, HW])
        s_bank = [ps(f"a_s{i}") for i in range(2)]
        t_bank = [ps(f"a_t{i}") for i in range(RING)]
        p_bank = [ps(f"a_p{i}") for i in range(2)]
        o_bank = ps("a_o")

        tab_in = sem("a_tab_in")
        ident_set, ident_done = sem("a_ident_set"), sem("a_ident_done")
        pad_set = sem("a_pad_set")
        ctx_loaded = [sem(f"a_ctx_loaded{i}") for i in range(CTX_SLOTS)]
        ctx_hi, ctx_lo = sem("a_ctx_hi"), sem("a_ctx_lo")
        mask_in = [sem(f"a_mask_in{t}") for t in range(QT)]
        q_in = [sem(f"a_q_in{t}") for t in range(QT)]
        wk_hi, wk_lo, wv_hi, wv_lo = sem("a_wk_hi"), sem("a_wk_lo"), sem("a_wv_hi"), sem("a_wv_lo")
        p_filled, vT_done = sem("a_p_filled"), sem("a_vT_done")
        k_mul, k_sum, k_hi, k_lo = sem("a_k_mul"), sem("a_k_sum"), sem("a_k_hi"), sem("a_k_lo")
        t_filled, t_hi, t_lo = sem("a_t_filled"), sem("a_t_hi"), sem("a_t_lo")
        s_filled, s_read = sem("a_s_filled"), sem("a_s_read")
        max_done, exp_done = sem("a_max_done"), sem("a_exp_done")
        sum_done, inv_done, rows_turned, rows_done = sem("a_sum_done"), sem("a_inv_done"), sem("a_rows_turned"), sem("a_rows_done")
        pv_done, o_done = sem("a_pv_done"), sem("a_o_done")
        dve_passed, pool_passed = sem("a_dve_passed"), sem("a_pool_passed")
        o_stored = [sem(f"a_o_stored{t}") for t in range(QT)]
        READ_CREDIT = 2
        TURN_CREDIT = 1
        O_CREDIT = 1
        BLK = 32

        VOFF = [TV, 0]
        STEPS = [v + KTILES for v in VOFF]
        SUM_AT = 4
        FIRST_AT, LAST_AT = [0, 1], [s - 1 for s in STEPS]
        chunks_at = [[[k for k in range(SCH) if FIRST_AT[t] + -(-k * (LAST_AT[t] - FIRST_AT[t]) // SCH) == i]
                      for i in range(STEPS[t])] for t in range(QT)]
        EXP_PARTS = [(0, 802), (802, SK)]
        exp_at = [[[] for _ in range(STEPS[t] + 1)] for t in range(QT)]
        for t in range(QT):
            for u in range(HPG):
                ready = next(i for i in range(STEPS[t]) if u * NCH + NCH - 1 in chunks_at[t][i])
                for part in range(2):
                    exp_at[t][min(ready + 2 + part, STEPS[t])].append((u, part))
        PIECES = NCH * DC

        def piece(q):
            (start, width, real), c = KCH[q // DC], q % DC
            return c, start, real

        def t_base(hg):
            return hg * TG + TURN_CREDIT

        def over_heads(eng, prologue, head):
            prologue()
            with eng.Fori(0, BATCH - 1) as b:
                with eng.Fori(0, KVH - 1) as g:
                    head(b, g, b * KVH + g, "inner")
                head(b, KVH - 1, b * KVH + KVH - 1, "next batch")
            with eng.Fori(0, KVH - 1) as g:
                head(BATCH - 1, g, g + (BATCH - 1) * KVH, "inner")
            head(BATCH - 1, KVH - 1, BATCH * KVH - 1, "end")

        block = ctx.enter_context(nc.Block())

        @block.sync
        def _(sp):
            def load_ctx(b, q):
                c, start, real = piece(q)
                sp.dma_start(ctx_raw[:, q % CTX_SLOTS, 0:real],
                             ctx_t[bass.ds(b, 1), c * P:(c + 1) * P, start:start + real].rearrange("o p k -> (o p) k")
                             ).then_inc(ctx_loaded[q % CTX_SLOTS], 16)

            def load_w(w, g):
                sp.dma_start(w_raw[:, :, :], w.rearrange("(c p) n -> p c n", p=P)[:, :, bass.ds(g * DH, DH)]).then_inc(w_in, 16)

            def load_q(b, g, t):
                src = q_scratch[bass.ds(g, 1), bass.ds(b * QT + t, 1), :, :].rearrange("a o p w -> (a o p) w")
                sp.dma_start(qT_hl[:, t, :, :].rearrange("p h w -> p (h w)").bitcast(F32), src.bitcast(F32)).then_inc(q_in[t], 16)

            def load_mask(b, t):
                sp.dma_start(mask_t[:, t, :], mask[bass.ds(b, 1), t * P:(t + 1) * P, :].rearrange("o p k -> (o p) k")
                             ).then_inc(mask_in[t], 16)

            def store_o(b, g, t):
                dst = o_scratch[bass.ds(g, 1), bass.ds(b * QT + t, 1), :, :].rearrange("a o p w -> (a o p) w")
                sp.dma_start(dst, oT[:, t, :]).then_inc(o_stored[t], 16)

            def prologue():
                for t in range(QT):
                    sp.sem_inc(o_stored[t], 16)
                sp.dma_start(cos_t[:, :], cos_k).then_inc(tab_in, 16)
                sp.dma_start(sin_t[:, :], sin_k).then_inc(tab_in, 16)
                load_mask(0, 0)
                sp.wait_ge(wk_lo, 1)
                load_w(wv, 0)
                sp.wait_ge(last_q_stored, Q_LAST)
                load_q(0, 0, 0)
                load_q(0, 0, 1)
                load_mask(0, 1)

            def head(b, g, hg, kind):
                if kind == "end":
                    sp.wait_ge(k_mul, BATCH * KVH * NCH)
                    for n in range(APK):
                        sp.dma_start(gates[n * RANK:(n + 1) * RANK, :, :],
                                     gate_t.rearrange("(k n) b -> n k b", n=APK)[n:n + 1, :, :].to_broadcast([RANK, NK, NT])
                                     ).then_inc(gates_in, 16)
                    sp.dma_start(a_raw, lora_a.rearrange("n r i -> (n r) i").rearrange("(k p) i -> p k i", p=P)).then_inc(a_in, 16)
                nb, ng = (b, g + 1) if kind == "inner" else (b + 1, 0)
                if kind != "end":
                    sp.wait_ge(wv_lo, hg + 1)
                    load_w(wk, ng)
                    sp.wait_ge(s_filled, (2 * hg + 1) * SCH)
                    load_q(nb, ng, 0)
                if kind == "next batch":
                    for q in range(CTX_SLOTS):
                        sp.wait_ge(ctx_lo, (b + 1) * PIECES)
                        load_ctx(nb, q)
                    sp.wait_ge(s_read, (2 * hg + 1) * SCH + READ_CREDIT)
                    load_mask(nb, 0)
                if kind != "end":
                    sp.wait_ge(wk_lo, hg + 2)
                    load_w(wv, ng)
                if kind == "next batch":
                    for q in range(CTX_SLOTS, PIECES):
                        sp.wait_ge(ctx_lo, nb * PIECES + q - CTX_SLOTS + 1)
                        load_ctx(nb, q)
                if kind != "end":
                    sp.wait_ge(s_filled, (2 * hg + 2) * SCH)
                    load_q(nb, ng, 1)
                if kind == "next batch":
                    sp.wait_ge(s_read, (2 * hg + 2) * SCH + READ_CREDIT)
                    load_mask(nb, 1)
                sp.wait_ge(o_done, hg * 2 + 1 + O_CREDIT)
                store_o(b, g, 0)
                sp.wait_ge(o_done, hg * 2 + 2 + O_CREDIT)
                store_o(b, g, 1)

            over_heads(sp, prologue, head)
            for t in range(QT):
                sp.wait_ge(o_stored[t], 16 * (BATCH * KVH + 1))

        @block.gpsimd
        def _(pool):
            def split(hl, hi, lo, hg, loads):
                pool.wait_ge(w_in, 16 * loads)
                pool.sem_inc(pool_passed, 1)
                pool.tensor_copy(hl[:, 0, :, :], w_raw[:, :, :]).then_inc(hi, 1)
                pool.wait_ge(hi, hg + 1)
                pool.tensor_tensor(out=hl[:, 1, :, :], in0=w_raw[:, :, :], in1=hl[:, 0, :, :].bitcast(F32),
                                   op=ALU.subtract).then_inc(lo, 1)

            def context(b, q):
                c, start, real = piece(q)
                pool.wait_ge(ctx_hi, b * PIECES + q + 1)
                pool.tensor_tensor(out=ctxT_hl[:, 1, c, start:start + real], in0=ctx_raw[:, q % CTX_SLOTS, 0:real],
                                   in1=ctxT_hl[:, 0, c, start:start + real].bitcast(F32), op=ALU.subtract).then_inc(ctx_lo, 1)

            def keys_lo(hg):
                for c, (start, width, _) in enumerate(KCH):
                    pool.wait_ge(k_hi, hg * NCH + c + 1)
                    pool.tensor_tensor(out=kT_hl[:, 1, start:start + width], in0=rot[:, c % 2, 0:width],
                                       in1=kT_hl[:, 0, start:start + width].bitcast(F32), op=ALU.subtract).then_inc(k_lo, 1)

            def prologue():
                pool.memset(ident[:, :], 0.0).then_inc(ident_set, 1)
                pool.wait_ge(ident_set, 1)
                pool.affine_select(out=ident[:, :], in_=ident[:, :], compare_op=ALU.not_equal, fill=1.0,
                                   base=0, pattern=[[-1, P]], channel_multiplier=1).then_inc(ident_done, 1)
                pool.memset(ctxT_hl[:, :, :, SK:SKP].bitcast(F32), 0.0).then_inc(pad_set, 1)
                keys_lo(0)
                split(wv_hl, wv_hi, wv_lo, 0, 2)

            def head(b, g, hg, kind):
                if kind != "end":
                    pool.wait_ge(p_filled, 2 * NCH * (hg + 1))
                    split(wk_hl, wk_hi, wk_lo, hg + 1, 2 * hg + 3)
                    if kind == "next batch":
                        for q in range(CTX_SLOTS):
                            context(b + 1, q)
                    split(wv_hl, wv_hi, wv_lo, hg + 1, 2 * hg + 4)
                    if kind == "next batch":
                        for q in range(CTX_SLOTS, PIECES):
                            context(b + 1, q)
                if kind != "end":
                    keys_lo(hg + 1)

            over_heads(pool, prologue, head)

        @block.scalar
        def _(act):
            def exps(n, t, u, part):
                lo, hi = EXP_PARTS[part]
                act.wait_ge(max_done, n * HPG + u + 1)
                act.activation(probs[t][:, u, lo:hi], probs[t][:, u, lo:hi], ACT.Exp, bias=neg_max[:, t, u:u + 1],
                               accum_out=part_sum[:, t, u, part:part + 1]).then_inc(exp_done, 1)

            def context(b, q):
                c, start, real = piece(q)
                act.wait_ge(ctx_loaded[q % CTX_SLOTS], 16 * ((b - 1) * (PIECES // CTX_SLOTS) + q // CTX_SLOTS + 1))
                act.activation(ctxT_hl[:, 0, c, start:start + real], ctx_raw[:, q % CTX_SLOTS, 0:real], ACT.Copy).then_inc(ctx_hi, 1)

            def high(n, T, t, i):
                act.wait_ge(t_filled, T + i + 1)
                bank, j = t_bank[i % RING], i - VOFF[t]
                if j < -1:
                    act.activation(v_hl[:, 0, 4 * i:4 * i + 4, :], bank[:, :].rearrange("p (j d) -> p j d", d=DH),
                                   ACT.Copy).then_inc(t_hi, 1)
                elif j == -1:
                    act.activation(v_hl[0:KREM, 0, KTILES - 1, :], bank[0:KREM, 0:DH], ACT.Copy).then_inc(t_hi, 1)
                else:
                    if j >= RING:
                        act.wait_ge(pv_done, n * KTILES + j - RING + 1)
                    rows = key_rows(j)
                    act.activation(pT_hl[0:rows, j % RING, 0, :], bank[0:rows, :], ACT.Copy).then_inc(t_hi, 1)

            def half(n, T, t, more, next_b, done=0):
                if not done:
                    high(n, T, t, 0)
                for i in range(STEPS[t]):
                    if done <= i + 1 < STEPS[t]:
                        high(n, T, t, i + 1)
                    if i == SUM_AT + 4:
                        act.wait_ge(rows_turned, (n + 1) * P // BLK)
                        for row in range(BLK, P, BLK):
                            act.activation(inv_rows[row:row + BLK, :, :], inv_rows[0:BLK, :, :], ACT.Copy).then_inc(rows_done, 1)
                    if more:
                        for u, part in exp_at[t][i]:
                            exps(n + 1, 1 - t, u, part)
                    if next_b is not None and i < PIECES:
                        context(next_b, i)
                if more:
                    for u, part in exp_at[t][STEPS[t]]:
                        exps(n + 1, 1 - t, u, part)

            def keys(hg, T=None):
                for c, (start, width, _) in enumerate(KCH):
                    if c == NCH - 2 and T is not None:
                        high(hg * 2 - 1, T, 1, 0)
                        high(hg * 2 - 1, T, 1, 1)
                    act.wait_ge(k_sum, hg * NCH + c + 1)
                    act.activation(kT_hl[:, 0, start:start + width], rot[:, c % 2, 0:width], ACT.Copy).then_inc(k_hi, 1)
                    if c == NCH - 2 and T is not None:
                        high(hg * 2 - 1, T, 1, 2)

            def values(hg):
                for c, (start, width, _) in enumerate(KCH):
                    act.wait_ge(p_filled, (2 * hg + 1) * NCH + c + 1)
                    act.activation(vT[:, start:start + width], p_bank[c % 2][:, 0:width], ACT.Copy).then_inc(vT_done, 1)

            def prologue():
                act.wait_ge(w_in, 16)
                act.activation(wk_hl[:, 0, :, :], w_raw[:, :, :], ACT.Copy).then_inc(wk_hi, 1)
                act.wait_ge(ctx_first_in, 16 * NCH)
                for start, _, real in KCH:
                    act.activation(ctxT_hl[:, 0, :, start:start + real], ctx_first[:, :, start:start + real],
                                   ACT.Copy).then_inc(ctx_hi, DC)
                keys(0)
                for u in range(HPG):
                    for part in range(2):
                        exps(0, 0, u, part)

            def head(b, g, hg, kind):
                T = t_base(hg)
                values(hg)
                half(hg * 2, T, 0, True, b + 1 if kind == "next batch" else None)
                if kind != "end":
                    keys(hg + 1, T + TV + TH)
                half(hg * 2 + 1, T + TV + TH, 1, kind != "end", None, done=3 if kind != "end" else 0)

            act.sem_inc(t_hi, TURN_CREDIT)
            over_heads(act, prologue, head)

        @block.vector
        def _(dve):
            def read_scores(n, t, k):
                u, c = divmod(k, NCH)
                start, _, width = KCH[c]
                dve.wait_ge(s_filled, n * SCH + k + 1)
                dve.sem_inc(dve_passed, 1)
                dve.tensor_tensor_reduce(out=probs[t][:, u, start:start + width], in0=s_bank[k % 2][:, 0:width],
                                         in1=mask_t[:, t, start:start + width], scale=1.0, scalar=NEG_HUGE,
                                         op0=ALU.add, op1=ALU.max, accum_out=chunk_max[:, t, u, c:c + 1]).then_inc(s_read, 1)
                if c == NCH - 1:
                    dve.wait_ge(s_read, n * SCH + k + 1 + READ_CREDIT)
                    dve.tensor_reduce(neg_max[:, t, u:u + 1], chunk_max[:, t, u, :], AX.X, ALU.max, negate=True).then_inc(max_done, 1)

            def low(T, t, i):
                dve.wait_ge(t_hi, T + i + 1)
                bank, j = t_bank[i % RING], i - VOFF[t]
                if j < -1:
                    high, dst = v_hl[:, 0, 4 * i:4 * i + 4, :], v_hl[:, 1, 4 * i:4 * i + 4, :]
                    src = bank[:, :].rearrange("p (j d) -> p j d", d=DH)
                elif j == -1:
                    high, dst = (v_hl[0:KREM, h, KTILES - 1, :] for h in range(2))
                    src = bank[0:KREM, 0:DH]
                else:
                    high, dst = (pT_hl[0:key_rows(j), j % RING, h, :] for h in range(2))
                    src = bank[0:key_rows(j), :]
                dve.tensor_tensor(out=dst, in0=src, in1=high.bitcast(F32), op=ALU.subtract).then_inc(t_lo, 1)

            def half(n, T, t, more, hg, b, next_b, done=0):
                for i in range(done, 2):
                    low(T, t, i)
                if more:
                    dve.wait_ge(mask_in[1 - t], 16 * ((next_b if t == 1 and next_b is not None else b) + 1))
                for i in range(STEPS[t]):
                    if 2 <= i + 1 < STEPS[t]:
                        low(T, t, i + 1)
                    if more:
                        for k in chunks_at[t][i]:
                            read_scores(n + 1, 1 - t, k)
                    if i == SUM_AT:
                        dve.wait_ge(exp_done, (n + 1) * HPG * 2)
                        dve.tensor_tensor(out=row_sum[:, :], in0=part_sum[:, t, :, 0], in1=part_sum[:, t, :, 1],
                                          op=ALU.add).then_inc(sum_done, 1)
                    if i == SUM_AT + 1:
                        dve.wait_ge(sum_done, n + 1)
                        dve.reciprocal(inv_sum[:, :], row_sum[:, :]).then_inc(inv_done, 1)
                    if i == SUM_AT + 2:
                        dve.wait_ge(inv_done, n + 1)
                        for row in range(0, P, BLK):
                            dve.sem_inc(dve_passed, 1)
                            dve.transpose(inv_rows[0:BLK, :, row:row + BLK],
                                          inv_sum[row:row + BLK, :].unsqueeze(2).to_broadcast([BLK, HPG, BLK])).then_inc(rows_turned, 1)
                dve.wait_ge(rows_done, (n + 1) * (P // BLK - 1))
                dve.wait_ge(pv_done, (n + 1) * KTILES)
                dve.wait_ge(o_stored[t], 16 * (hg + 1))
                dve.tensor_tensor(out=oT[:, t, :], in0=o_bank[:, :],
                                  in1=inv_rows[:, :, :].rearrange("p u q -> p (u q)"), op=ALU.mult).then_inc(o_done, 1)

            def keys(hg, T=None):
                for c, (start, width, _) in enumerate(KCH):
                    i = hg * NCH + c
                    if c == NCH - 1 and T is not None:
                        low(T, 1, 0)
                        low(T, 1, 1)
                    bank, r = p_bank[c % 2], c % 2
                    dve.wait_ge(p_filled, hg * 2 * NCH + c + 1)
                    if T is not None or c >= 2:
                        dve.wait_ge(k_lo, i - 1)
                    cols = slice(start, start + width)
                    dve.tensor_tensor(out=rot[0:64, r, 0:width], in0=bank[64:128, 0:width], in1=sin_t[64:128, cols], op=ALU.mult)
                    dve.tensor_tensor(out=rot[64:128, r, 0:width], in0=bank[0:64, 0:width], in1=sin_t[0:64, cols], op=ALU.mult)
                    dve.tensor_tensor(out=straight[:, r, 0:width], in0=bank[:, 0:width], in1=cos_t[:, cols], op=ALU.mult).then_inc(k_mul, 1)
                    dve.wait_ge(k_mul, i + 1)
                    dve.tensor_tensor(out=rot[:, r, 0:width], in0=rot[:, r, 0:width], in1=straight[:, r, 0:width],
                                      op=ALU.add).then_inc(k_sum, 1)

            def prologue():
                dve.sem_inc(s_read, READ_CREDIT)
                dve.sem_inc(t_lo, TURN_CREDIT)
                dve.sem_inc(o_done, O_CREDIT)
                dve.wait_ge(wk_hi, 1)
                dve.tensor_tensor(out=wk_hl[:, 1, :, :], in0=w_raw[:, :, :], in1=wk_hl[:, 0, :, :].bitcast(F32),
                                  op=ALU.subtract).then_inc(wk_lo, 1)
                for c, (start, _, real) in enumerate(KCH):
                    dve.wait_ge(ctx_hi, (c + 1) * DC)
                    dve.tensor_tensor(out=ctxT_hl[:, 1, :, start:start + real], in0=ctx_first[:, :, start:start + real],
                                      in1=ctxT_hl[:, 0, :, start:start + real].bitcast(F32), op=ALU.subtract).then_inc(ctx_lo, DC)
                dve.wait_ge(tab_in, 32)
                keys(0)
                dve.wait_ge(mask_in[0], 16)
                dve.wait_ge(last_q_stored, Q_LAST)
                for k in range(SCH):
                    read_scores(0, 0, k)

            def head(b, g, hg, kind):
                T = t_base(hg)
                next_b = b + 1 if kind == "next batch" else None
                half(hg * 2, T, 0, True, hg, b, next_b)
                if kind != "end":
                    keys(hg + 1, T + TV + TH)
                half(hg * 2 + 1, T + TV + TH, 1, kind != "end", hg, b, next_b, done=2 if kind != "end" else 0)

            over_heads(dve, prologue, head)

        @block.tensor
        def _(pe):
            def project(w_hl, bank, start, width):
                steps = [(a, b, k) for a, b in PARTS for k in range(DC)]
                for a, b, k in steps:
                    last = pe.matmul(bank[:, 0:width], w_hl[:, a, k, :], ctxT_hl[:, b, k, start:start + width],
                                     start=(a, b, k) == steps[0], stop=(a, b, k) == steps[-1])
                last.then_inc(p_filled, 1)

            def keys(hg, b, T=None):
                pe.wait_ge(wk_lo, hg + 1)
                if T is not None:
                    pe.wait_ge(ctx_lo, (b + 1) * PIECES)
                for c, (start, width, _) in enumerate(KCH):
                    if T is None:
                        pe.wait_ge(ctx_lo, (c + 1) * DC)
                    if c == NCH - 1 and T is not None:
                        fill(hg * 2 - 1, T, 1, 0, hg - 1)
                        fill(hg * 2 - 1, T, 1, 1, hg - 1)
                    if c >= 2:
                        pe.wait_ge(k_mul, hg * NCH + c - 1)
                    project(wk_hl, p_bank[c % 2], start, width)

            def values(hg):
                pe.wait_ge(wv_lo, hg + 1)
                for c, (start, width, _) in enumerate(KCH):
                    if c < 2:
                        pe.wait_ge(k_mul, hg * NCH + c + 3)
                    else:
                        pe.wait_ge(vT_done, hg * NCH + c - 1)
                    project(wv_hl, p_bank[c % 2], start, width)

            def scores(n, t, k):
                u, c = divmod(k, NCH)
                start, width, _ = KCH[c]
                pe.wait_ge(s_read, n * SCH + k - 1 + READ_CREDIT)
                for i, (a, b) in enumerate(PARTS):
                    last = pe.matmul(s_bank[k % 2][:, 0:width], qT_hl[:, t, a, u * P:(u + 1) * P],
                                     kT_hl[:, b, start:start + width], start=i == 0, stop=i == 2)
                last.then_inc(s_filled, 1)

            def fill(n, T, t, i, hg):
                pe.wait_ge(t_lo, T + max(0, i - RING + 1))
                bank, j = t_bank[i % RING], i - VOFF[t]
                if j < 0:
                    tiles = range(4 * i, min(4 * i + 4, KTILES))
                    pe.wait_ge(vT_done, hg * NCH + sum(start < (tiles[-1] + 1) * P for start, _, _ in KCH))
                    for v in tiles:
                        rows = key_rows(v)
                        last = pe.transpose(bank[0:rows, (v % 4) * P:(v % 4 + 1) * P], vT[:, v * P:v * P + rows], ident[:, :])
                else:
                    if j == 0:
                        pe.wait_ge(exp_done, (n + 1) * HPG * 2)
                    rows = key_rows(j)
                    for u in range(HPG):
                        last = pe.transpose(bank[0:rows, u * P:(u + 1) * P], probs[t][:, u, j * P:j * P + rows], ident[:, :])
                last.then_inc(t_filled, 1)

            def half(n, T, t, more, hg, done=0):
                for i in range(done, 2):
                    fill(n, T, t, i, hg)
                for i in range(STEPS[t]):
                    if i + 2 < STEPS[t]:
                        fill(n, T, t, i + 2, hg)
                    if more:
                        for k in chunks_at[t][i]:
                            if k == 0:
                                pe.wait_ge(q_in[1 - t], 16 * (hg + 1 + t))
                            if t == 1 and k < NCH:
                                pe.wait_ge(k_lo, (hg + 1) * NCH + k + 1)
                            scores(n + 1, 1 - t, k)
                    j = i - VOFF[t]
                    if j >= 0:
                        rows = key_rows(j)
                        if j == 0:
                            pe.wait_ge(o_done, n + O_CREDIT)
                        pe.wait_ge(t_lo, T + i + 1)
                        for p, (a, b) in enumerate(PARTS):
                            last = pe.matmul(o_bank[:, :], v_hl[0:rows, a, j, :], pT_hl[0:rows, j % RING, b, :],
                                             start=j == 0 and p == 0, stop=j == KTILES - 1 and p == 2)
                        last.then_inc(pv_done, 1)

            def prologue():
                pe.sem_inc(t_filled, TURN_CREDIT)
                pe.wait_ge(ident_done, 1)
                pe.wait_ge(pad_set, 1)
                keys(0, 0)
                pe.wait_ge(q_in[0], 16)
                for k in range(SCH):
                    if k < NCH:
                        pe.wait_ge(k_lo, k + 1)
                    scores(0, 0, k)

            def head(b, g, hg, kind):
                T = t_base(hg)
                values(hg)
                half(hg * 2, T, 0, True, hg)
                if kind != "end":
                    keys(hg + 1, b + 1 if kind == "next batch" else b, T + TV + TH)
                half(hg * 2 + 1, T + TV + TH, 1, kind != "end", hg, done=2 if kind != "end" else 0)

            over_heads(pe, prologue, head)


def output_stage(nc, sem, x, wo, kern, bias, gate_t, lora_a, lora_b_t, a_shared_t, b_shared_t, o_scratch, out,
                 probs_1, w_raw_1, tables, gates, a_raw, gates_in, a_in):
    ORDER = [4, 5, 6, 7, 0, 1, 2, 3]
    HALF = NT // 2
    LAST = KVH - 1
    with ExitStack() as ctx:
        sb = lambda name, shape, dt=F32: ctx.enter_context(nc.sbuf_tensor(name, shape, dt))
        w_raw = sb("p_w_raw", [P, 2, HPG, DM])
        w_hl = sb("p_w_hl", [P, 2, 2, HPG, DM], F32R)
        o_raw = sb("p_o_raw", [P, 2, NT, HW])
        o_hl = sb("p_o_hl", [P, 2, 2, NT, HW], F32R)
        xt = probs_1[:, :, :].rearrange("p u k -> p (u k)")[:, 0:NT * DM].rearrange("p (n d) -> p n d", d=DM)
        ident = sb("p_ident", [P, P])
        diag = sb("p_diag", [P, RANK])
        bias_rows = w_raw_1[:, :, :].rearrange("p c n -> p (c n)")
        G = tables[:, :, :].rearrange("p t k -> p (t k)")[:, NK * DM + NK * NT:NK * (DM + NT + NT * RANK)].rearrange(
            "p (k b r) -> p k b r", b=NT, r=RANK)
        rest = probs_1[:, :, :].rearrange("p u k -> p (u k)")[:, NT * DM:NT * DM + DC * RANK + DM]
        asT_raw = rest[:, 0:DC * RANK].rearrange("p (c r) -> p c r", r=RANK)
        bsT_raw = rest[0:RANK, DC * RANK:DC * RANK + DM]
        asT_hl = sb("p_asT_hl", [P, 2, DC, RANK], F32R)
        bsT_hl = sb("p_bsT_hl", [RANK, 2, DM], F32R)
        aT_hl = sb("p_aT_hl", [P, 2, DC, NT * RANK], F32R)
        bT_hl = sb("p_bT_hl", [P, 2, 2, DM], F32R)
        stats = sb("p_stats", [P, NT, 6])
        mean_var = sb("p_mean_var", [P, NT, 2])
        var_eps = sb("p_var_eps", [P, NT])
        minus_half = sb("p_minus_half", [P, 1])
        rstd = sb("p_rstd", [P, NT])
        bT_raw = o_raw[:, 1, HALF:NT, :]
        xn = o_raw[:, 0, :, :]
        y = o_raw[:, 1, :, :]
        xT_hl = o_hl[:, 0, :, :, :]
        k_hl = w_hl[:, 0, :, :, :]
        ax_hl = w_hl[:, 1, :, 0:2, :]
        axs_hl = w_hl[0:RANK, 1, :, 2:4, :]
        acc = [ctx.enter_context(nc.psum_tensor(f"p_acc{n}", [P, DM], F32)) for n in range(NT)]

        x_in, bias_in, b_in = sem("p_x_in"), sem("p_bias_in"), sem("p_b_in")
        w_in = [sem(f"p_w_in{s}") for s in range(2)]
        o_in = [sem(f"p_o_in{s}") for s in range(2)]
        shared_in = sem("p_shared_in")
        ident_set, ident_done, half_set, zeroed = sem("p_ident_set"), sem("p_ident_done"), sem("p_half_set"), sem("p_zeroed")
        diag_done, G_done = sem("p_diag_done"), sem("p_G_done")
        shared_hi, shared_lo = sem("p_shared_hi"), sem("p_shared_lo")
        lora_filled, lora_hi, lora_lo = sem("p_lora_filled"), sem("p_lora_hi"), sem("p_lora_lo")
        w_hi, w_lo, o_hi, o_lo = sem("p_w_hi"), sem("p_w_lo"), sem("p_o_hi"), sem("p_o_lo")
        tile_done = sem("p_tile_done")
        x2_done, stat_done, aggr_done, veps_done = sem("p_x2_done"), sem("p_stat_done"), sem("p_aggr_done"), sem("p_veps_done")
        rstd_done, xn_done, xb_done = sem("p_rstd_done"), sem("p_xn_done"), sem("p_xb_done")
        xT_filled, xT_hi, xT_lo = sem("p_xT_filled"), sem("p_xT_hi"), sem("p_xT_lo")
        ax_filled, ax_hi, ax_lo = sem("p_ax_filled"), sem("p_ax_hi"), sem("p_ax_lo")
        y_filled, y_done, stored = sem("p_y_filled"), sem("p_y_done"), sem("p_stored")

        def lora_fills():
            for i in range(2):
                yield acc[i][:, :].rearrange("p (c m) -> p c m", c=2), [aT_hl[:, h, 2 * i:2 * i + 2, :] for h in range(2)]
            for i in range(2):
                yield acc[2 + i][:, :], [bT_hl[:, h, i, :] for h in range(2)]

        def ax_fills(half):
            for q in range(APK):
                rows, cols = slice(q * RANK, (q + 1) * RANK), slice(q * P, (q + 1) * P)
                yield acc[0][rows, cols], [ax_hl[rows, h, half, cols] for h in range(2)]
            yield acc[1][0:RANK, :], [axs_hl[:, h, half, :] for h in range(2)]

        AX_PARTS = APK + 1
        Y_BANK = [4, 5, 6, 7, 2, 3, 4, 5]
        block = ctx.enter_context(nc.Block())

        @block.sync
        def _(sp):
            def load_w(src, s):
                sp.dma_start(w_raw[:, s, :, :], src).then_inc(w_in[s], 16)

            def load_group(group, s):
                load_w(wo.rearrange("(g h p) n -> g p h n", p=P, h=HPG)[bass.ds(group, 1), :, :, :].rearrange("o p h n -> (o p) h n"), s)
                sp.dma_start(o_raw[:, s, :, :], o_scratch[bass.ds(group, 1), :, :, :].rearrange("o n p w -> p (o n) w")).then_inc(o_in[s], 16)

            sp.dma_start(bT_raw, lora_b_t.rearrange("n r o -> (n r) o").rearrange("(k p) o -> p k o", p=P)).then_inc(b_in, 16)
            load_group(0, 0)
            sp.dma_start(asT_raw, a_shared_t.rearrange("(c p) r -> p c r", p=P)).then_inc(shared_in, 16)
            sp.dma_start(bsT_raw, b_shared_t).then_inc(shared_in, 16)
            sp.wait_ge(lora_filled, 4)
            load_group(1, 1)
            sp.dma_start(xt[:, :, :], x.rearrange("b (t p) d -> p (b t) d", p=P)).then_inc(x_in, 16)
            sp.dma_start(bias_rows[:, :], bias.rearrange("(o n) -> o n", o=1).to_broadcast([P, DM])).then_inc(bias_in, 16)
            with sp.Fori(0, KVH // 2 - 1) as pair:
                for s in range(2):
                    sp.wait_ge(o_lo, pair * 4 + s * 2 + 2)
                    load_group(pair * 2 + s + 2, s)
            sp.wait_ge(w_lo, LAST)
            load_w(kern.rearrange("(c p) n -> p c n", p=P), 0)
            out_v = out.rearrange("b (t p) d -> (b t) p d", p=P)
            for i, n in enumerate(ORDER):
                sp.wait_ge(y_done, i + 1)
                sp.dma_start(out_v[n, :, :], y[:, n, :]).then_inc(stored, 16)
            sp.wait_ge(stored, 16 * NT)

        @block.gpsimd
        def _(pool):
            pool.memset(ident[:, :], 0.0).then_inc(ident_set, 1)
            pool.memset(minus_half[:, :], -0.5).then_inc(half_set, 1)
            pool.wait_ge(ident_set, 1)
            pool.affine_select(out=ident[:, :], in_=ident[:, :], compare_op=ALU.not_equal, fill=1.0,
                               base=0, pattern=[[-1, P]], channel_multiplier=1).then_inc(ident_done, 1)
            pool.wait_ge(half_set, 1)
            pool.wait_ge(bias_in, 16)

            def add_bias(i):
                pool.wait_ge(xn_done, i + 1)
                n = ORDER[i]
                pool.tensor_tensor(out=xt[:, n, :], in0=xt[:, n, :], in1=bias_rows[:, :], op=ALU.add).then_inc(xb_done, 1)

            for i, n in enumerate(ORDER):
                pool.wait_ge(veps_done, i + 1)
                pool.tensor_tensor(out=rstd[:, n:n + 1], in0=var_eps[:, n:n + 1], in1=minus_half[:, :], op=ALU.pow).then_inc(rstd_done, 1)
                if i >= 2:
                    add_bias(i - 2)
            pool.wait_ge(tile_done, KVH * NT)
            pool.memset(ax_hl.bitcast(F32), 0.0).then_inc(zeroed, 1)
            add_bias(NT - 2)
            add_bias(NT - 1)

        @block.scalar
        def _(act):
            def high(src, dst, done):
                act.activation(dst, src, ACT.Copy).then_inc(done, 1)

            def weights(group, s, turn, free=None):
                if free is not None:
                    act.wait_ge(tile_done, free)
                act.wait_ge(w_in[s], 16 * (turn + 1))
                high(w_raw[:, s, :, :], w_hl[:, s, 0, :, :], w_hi)

            def heads(s, turn):
                act.wait_ge(o_in[s], 16 * (turn + 1))
                for tiles in (slice(HALF, NT), slice(0, HALF)):
                    high(o_raw[:, s, tiles, :], o_hl[:, s, 0, tiles, :], o_hi)

            weights(0, 0, 0)
            heads(0, 0)
            for i, (src, (dst, _)) in enumerate(lora_fills()):
                act.wait_ge(lora_filled, i + 1)
                high(src, dst, lora_hi)
            act.wait_ge(shared_in, 16 * 2)
            high(asT_raw, asT_hl[:, 0, :, :], shared_hi)
            high(bsT_raw, bsT_hl[:, 0, :], shared_hi)
            weights(1, 1, 0)
            heads(1, 0)
            with act.Fori(1, KVH // 2) as pair:
                for s in range(2):
                    weights(pair * 2 + s, s, pair, (pair * 2 + s - 1) * NT)
                    heads(s, pair)
            weights(KVH, 0, KVH // 2, LAST * NT)
            for i, n in enumerate(ORDER):
                act.wait_ge(xT_filled, i + 1)
                high(acc[n][:, :], xT_hl[:, 0, n, :], xT_hi)
                if i == NT - 1:
                    act.wait_ge(zeroed, 1)
                    for p, (src, (dst, _)) in enumerate(ax_fills(1)):
                        act.wait_ge(ax_filled, 1 + p // APK)
                        high(src, dst, ax_hi)
            for p, (src, (dst, _)) in enumerate(ax_fills(0)):
                act.wait_ge(ax_filled, 3 + p // APK)
                high(src, dst, ax_hi)

        @block.vector
        def _(dve):
            def low(raw, parts, done):
                dve.tensor_tensor(out=parts[1], in0=raw, in1=parts[0].bitcast(F32), op=ALU.subtract).then_inc(done, 1)

            def group(g, s):
                dve.wait_ge(w_hi, g + 1)
                low(w_raw[:, s, :, :], [w_hl[:, s, h, :, :] for h in range(2)], w_lo)
                for i, tiles in enumerate((slice(HALF, NT), slice(0, HALF))):
                    dve.wait_ge(o_hi, 2 * g + i + 1)
                    low(o_raw[:, s, tiles, :], [o_hl[:, s, h, tiles, :] for h in range(2)], o_lo)

            dve.wait_ge(ident_done, 1)
            for n in range(APK):
                rows = slice(n * RANK, (n + 1) * RANK)
                dve.tensor_copy(diag[rows, :], ident[rows, rows]).then_inc(diag_done, 1)
            dve.wait_ge(diag_done, APK)
            dve.wait_ge(gates_in, 16 * APK)
            dve.tensor_tensor(out=G[:, :, :, :].rearrange("p k b r -> p (k b) r"),
                              in0=gates[:, :, :].rearrange("p k b -> p (k b)").unsqueeze(2).to_broadcast([P, NK * NT, RANK]),
                              in1=diag[:, :].unsqueeze(1).to_broadcast([P, NK * NT, RANK]), op=ALU.mult).then_inc(G_done, 1)
            group(0, 0)
            for i, (src, parts) in enumerate(lora_fills()):
                dve.wait_ge(lora_hi, i + 1)
                low(src, parts, lora_lo)
            dve.wait_ge(shared_hi, 2)
            low(asT_raw, [asT_hl[:, h, :, :] for h in range(2)], shared_lo)
            low(bsT_raw, [bsT_hl[:, h, :] for h in range(2)], shared_lo)
            group(1, 1)
            with dve.Fori(1, KVH // 2) as pair:
                for s in range(2):
                    group(pair * 2 + s, s)

            def norm_start(i):
                n = ORDER[i]
                dve.wait_ge(tile_done, LAST * NT + i + 1)
                dve.tensor_tensor(out=xt[:, n, :], in0=acc[n][:, :], in1=xt[:, n, :], op=ALU.add).then_inc(x2_done, 1)
                dve.wait_ge(x2_done, i + 1)
                dve.bn_stats(stats[:, n, :], xt[:, n, :]).then_inc(stat_done, 1)
                dve.wait_ge(stat_done, i + 1)
                dve.bn_aggr(mean_var[:, n, :], stats[:, n, :]).then_inc(aggr_done, 1)
                dve.wait_ge(aggr_done, i + 1)
                dve.tensor_scalar(var_eps[:, n:n + 1], mean_var[:, n, 1:2], EPS, None, ALU.add).then_inc(veps_done, 1)

            def norm_end(i):
                n = ORDER[i]
                dve.wait_ge(rstd_done, i + 1)
                dve.tensor_scalar(xn[:, n, :], xt[:, n, :], mean_var[:, n, 0:1], rstd[:, n:n + 1],
                                  ALU.subtract, ALU.mult).then_inc(xn_done, 1)

            def turned_low(i):
                n = ORDER[i]
                dve.wait_ge(xT_hi, i + 1)
                low(acc[n][:, :], [xT_hl[:, h, n, :] for h in range(2)], xT_lo)

            def ax_low(half, first):
                for p, (src, parts) in enumerate(ax_fills(half)):
                    dve.wait_ge(ax_hi, first + p + 1)
                    low(src, parts, ax_lo)

            dve.wait_ge(w_hi, KVH + 1)
            low(w_raw[:, 0, :, :], [k_hl[:, h, :, :] for h in range(2)], w_lo)
            dve.wait_ge(x_in, 16)
            for i in range(NT + 3):
                if i < NT:
                    norm_start(i)
                if 1 <= i < NT + 1:
                    norm_end(i - 1)
                if i >= 3:
                    turned_low(i - 3)
            ax_low(1, 0)
            for i, n in enumerate(ORDER):
                if i == HALF:
                    ax_low(0, AX_PARTS)
                dve.wait_ge(y_filled, i + 1)
                dve.wait_ge(xb_done, i + 1)
                dve.tensor_tensor(out=y[:, n, :], in0=acc[Y_BANK[i]][:, :], in1=xt[:, n, :], op=ALU.add).then_inc(y_done, 1)

        @block.tensor
        def _(pe):
            def three(dst, stationary, moving, start=True, stop=True):
                for i, (a, b) in enumerate(PARTS):
                    last = pe.matmul(dst, stationary(a), moving(b), start=start and i == 0, stop=stop and i == 2)
                return last

            def tile(g, s, i, first=False, final=False):
                n = ORDER[i]
                if i == 0:
                    pe.wait_ge(w_lo, g + 1)
                if i % HALF == 0:
                    pe.wait_ge(o_lo, 2 * g + 1 + i // HALF)
                if first and i == HALF:
                    pe.wait_ge(lora_lo, 4)
                for hh in range(HPG):
                    last = three(acc[n][:, :], lambda h: o_hl[:, s, h, n, hh * P:(hh + 1) * P],
                                 lambda h: w_hl[:, s, h, hh, :], start=first and hh == 0, stop=final and hh == HPG - 1)
                last.then_inc(tile_done, 1)

            def turn(i):
                n = ORDER[i]
                pe.wait_ge(xn_done, i + 1)
                for c in range(DC):
                    last = pe.transpose(acc[n][:, c * P:(c + 1) * P], xn[:, n, c * P:(c + 1) * P], ident[:, :])
                last.then_inc(xT_filled, 1)

            def ax(half, turned, drained):
                pe.wait_ge(xT_lo, turned)
                if drained:
                    pe.wait_ge(ax_lo, drained)
                tiles = slice(half * HALF, (half + 1) * HALF)
                for c in range(DC):
                    last = three(acc[0][:, :], lambda h: aT_hl[:, h, c, half * P:(half + 1) * P],
                                 lambda h: xT_hl[:, h, tiles, c * P:(c + 1) * P], start=c == 0, stop=c == DC - 1)
                last.then_inc(ax_filled, 1)
                for c in range(DC):
                    last = three(acc[1][0:RANK, :], lambda h: asT_hl[:, h, c, :],
                                 lambda h: xT_hl[:, h, tiles, c * P:(c + 1) * P], start=c == 0, stop=c == DC - 1)
                last.then_inc(ax_filled, 1)

            def base(i):
                n, bank = ORDER[i], acc[Y_BANK[i]]
                if i == 0:
                    pe.wait_ge(w_lo, KVH + 1)
                if i < HALF:
                    pe.wait_ge(xT_lo, i + 1)
                elif i < HALF + 2:
                    pe.wait_ge(xT_lo, i + 3)
                else:
                    pe.wait_ge(y_done, i - HALF - 1)
                for c in range(DC):
                    three(bank[:, :], lambda h: xT_hl[:, h, n, c * P:(c + 1) * P], lambda h: k_hl[:, h, c, :],
                          start=c == 0, stop=False)

            def deltas(i):
                n, bank = ORDER[i], acc[Y_BANK[i]]
                half, cols = n // HALF, slice(n % HALF * P, (n % HALF + 1) * P)
                pe.wait_ge(ax_lo, AX_PARTS * (i // HALF + 1))
                three(bank[:, :], lambda h: ax_hl[:, h, half, cols], lambda h: bT_hl[:, h, half, :], start=False, stop=False)
                last = three(bank[:, :], lambda h: axs_hl[:, h, half, cols], lambda h: bsT_hl[:, h, :], start=False)
                last.then_inc(y_filled, 1)

            pe.wait_ge(G_done, 1)
            pe.wait_ge(a_in, 16)
            for i in range(2):
                for cc in range(2):
                    c = 2 * i + cc
                    for k in range(NK):
                        last = pe.matmul(acc[i][:, cc * 256:(cc + 1) * 256], a_raw[:, k, c * P:(c + 1) * P],
                                         G[:, k, :, :].rearrange("p b r -> p (b r)"), start=k == 0, stop=k == NK - 1)
                last.then_inc(lora_filled, 1)
            pe.wait_ge(b_in, 16)
            for i in range(2):
                for k in range(NK):
                    last = pe.matmul(acc[2 + i][:, :], G[:, k, i * APK:(i + 1) * APK, :].rearrange("p b r -> p (b r)"),
                                     bT_raw[:, k, :], start=k == 0, stop=k == NK - 1)
                last.then_inc(lora_filled, 1)
            for s in range(2):
                for i in range(NT):
                    tile(s, s, i, first=s == 0)
            with pe.Fori(1, KVH // 2 - 1) as pair:
                for s in range(2):
                    for i in range(NT):
                        tile(pair * 2 + s, s, i)
            for i in range(NT):
                tile(LAST - 1, 0, i)
            for i in range(NT):
                tile(LAST, 1, i, final=True)
                if i >= 2:
                    turn(i - 2)
            base(0)
            base(1)
            turn(NT - 2)
            base(2)
            turn(NT - 1)
            base(3)
            pe.wait_ge(shared_lo, 2)
            ax(1, HALF + 2, 0)
            base(4)
            base(5)
            for i in range(HALF):
                deltas(i)
            ax(0, NT, AX_PARTS)
            base(6)
            base(7)
            for i in range(HALF, NT):
                deltas(i)


def program(nc, x, ctx_t, mask, wq, wk, wv, wo, gate_t, kern, bias, lora_a, lora_b_t, a_shared_t, b_shared_t,
            cos_q, sin_q, cos_k, sin_k, out):
    with ExitStack() as ctx:
        sem = lambda name: ctx.enter_context(nc.semaphore(name))
        q_scratch = nc.dram_tensor("q_scratch", (KVH, NT, P, 2 * HW), F32R, kind="Internal").ap()
        o_scratch = nc.dram_tensor("o_scratch", (KVH, NT, P, HW), F32, kind="Internal").ap()
        probs_1 = ctx.enter_context(nc.sbuf_tensor("probs_1", [P, HPG, SK], F32))
        w_raw = ctx.enter_context(nc.sbuf_tensor("w_raw", [P, DC, DH], F32))
        ctx_first_in, w_in = sem("ctx_first_in"), sem("w_in")
        q_stored = [sem(f"q_stored{i}") for i in range(2)]
        query_stage(nc, sem, x, wq, cos_q, sin_q, q_scratch, ctx_t, wk, probs_1, w_raw, ctx_first_in, w_in, q_stored)
        tables = ctx.enter_context(nc.sbuf_tensor("tables", [P, 2, SKP], F32))
        flat = tables[:, :, :].rearrange("p t k -> p (t k)")
        a_raw = flat[:, 0:NK * DM].rearrange("p (k i) -> p k i", i=DM)
        gates = flat[:, NK * DM:NK * DM + NK * NT].rearrange("p (k b) -> p k b", b=NT)
        gates_in, a_in = sem("gates_in"), sem("a_in")
        attention_stage(nc, sem, ctx_t, mask, wk, wv, cos_k, sin_k, q_scratch, o_scratch, probs_1, w_raw, ctx_first_in, w_in,
                        q_stored[1], tables, gate_t, lora_a, gates, a_raw, gates_in, a_in)
        output_stage(nc, sem, x, wo, kern, bias, gate_t, lora_a, lora_b_t, a_shared_t, b_shared_t, o_scratch, out,
                     probs_1, w_raw, tables, gates, a_raw, gates_in, a_in)


def rotary_tables(np):
    f = np.float32
    inv_freq = f(1.0) / np.power(f(10000.0), np.arange(0, DH, 2, dtype=f) / f(DH))
    angle = np.arange(SKP, dtype=f)[None, :] * inv_freq[:, None]
    cos, sin = np.cos(angle.astype(np.float64)), np.sin(angle.astype(np.float64))
    cos, sin = np.concatenate([cos, cos]), np.concatenate([sin, -sin])
    scale = 1.0 / np.sqrt(float(DH))
    q = lambda a: np.tile(a[:, :SQ] * scale, (1, 512 // SQ)).astype(f)
    return q(cos), q(sin), cos.astype(f), sin.astype(f)


_INS = ["x", "ctx_4096", "mask_BxSxS2_ff0", "L0_xattn_wq", "L0_xattn_wk", "L0_xattn_wv", "L0_xattn_wo",
        "L0_ffn_gate", "L0_ffn_kernel", "L0_ffn_bias", "L0_ffn_lora_A", "L0_ffn_lora_B",
        "L0_ffn_lora_A_shared", "L0_ffn_lora_B_shared"]
_TABLES = ["cos_q", "sin_q", "cos_k", "sin_k"]


def kernel(**inputs):
    import numpy as np
    import concourse.bacc as bacc
    from concourse.bass_utils import run_bass_kernel_spmd

    nc = bacc.Bacc("TRN2", target_bir_lowering=False, num_devices=1)
    arrays, args = {}, []
    lay = {"ctx_4096": (0, 2, 1), "L0_ffn_gate": (1, 0), "L0_ffn_lora_B": (0, 2, 1), "L0_ffn_lora_A_shared": (1, 0), "L0_ffn_lora_B_shared": (1, 0)}
    named = [(n, np.ascontiguousarray(np.transpose(inputs[n], lay.get(n, range(np.ndim(inputs[n])))))) for n in _INS] + list(zip(_TABLES, rotary_tables(np)))
    for name, a in named:
        arrays[f"in_{name}"] = a
        args.append(nc.dram_tensor(f"in_{name}", a.shape, mybir.dt.from_np(a.dtype), kind="ExternalInput").ap())
    args.append(nc.dram_tensor("out", (BATCH, SQ, DM), F32, kind="ExternalOutput").ap())
    program(nc, *args)
    r = run_bass_kernel_spmd(nc, [arrays], core_ids=[0])
    return r.results[0]["out"]
```
